# Optimizing a Trainium2 kernel written in Bass

```python
import numpy as np
import jax
import jax.numpy as jnp

def _softmax(x, axis=-1):
    return jax.nn.softmax(x, axis=axis)

def _gelu(x):
    return jax.nn.gelu(x, approximate=True)

def _silu(x):
    return jax.nn.silu(x)

def _sigmoid(x):
    return jax.nn.sigmoid(x)

def _layernorm(x, axis=-1, eps=1e-05):
    m = jnp.mean(x, axis=axis, keepdims=True)
    v = jnp.var(x, axis=axis, keepdims=True)
    return (x - m) / jnp.sqrt(v + eps)

def _scatter_add(tgt, idx, src, axis=0):
    return tgt.at[idx].add(src)

def _segment_sum(src, seg, n):
    return jax.ops.segment_sum(src, seg, n)
kernel_name = 'mk_adaln_ffn_d1_seqx_r4_c95fc1'

def setup_inputs(seed: int=0):
    np.random.seed(seed)
    _w = jnp.asarray

    def _rec_inputs():
        import jax
        import jax.numpy as jnp
        _rk = jax.random.key(seed)
        x = -0.0003929 + 0.9999 * jax.random.normal(jax.random.fold_in(_rk, 1), (32, 64, 1024), jnp.float32)
        _lenS = 64 - jax.random.randint(jax.random.fold_in(_rk, 7), (32,), 0, max(1, 64 // 4) + 1, jnp.int32)
        _lenS2 = 64 - jax.random.randint(jax.random.fold_in(_rk, 8), (32,), 0, max(1, 64 // 4) + 1, jnp.int32)
        itok_B_8_3872 = jax.random.randint(jax.random.fold_in(_rk, 11), (32,), 8, 3873, jnp.int32)
        return (x, itok_B_8_3872)
    x, itok_B_8_3872 = _rec_inputs()

    def _L0_cond_setup():
        import math
        import jax, jax.numpy as jnp
        import numpy as np
        H, N, B, L = (64, 64, 16, 1024)
        DT_MIN, DT_MAX = (0.001, 0.1)

        def _get_kernel(log_dt, C, log_A_real, A_imag, length):
            Cc = C[..., 0] + 1j * C[..., 1]
            dt = jnp.exp(log_dt)
            A = -jnp.exp(log_A_real) + 1j * A_imag
            dtA = A * dt[:, None]
            P = dtA[:, :, None] * jnp.arange(length, dtype=jnp.float32)
            Cs = Cc * (jnp.exp(dtA) - 1.0) / A
            K = 2.0 * jnp.einsum('hn,hnl->hl', Cs, jnp.exp(P)).real
            return K
        key = jax.random.key(seed)
        ks = jax.random.split(key, 6)
        u = jax.random.normal(ks[0], (B, H, L), dtype=jnp.float32)
        length = jax.random.randint(ks[1], (B,), 0, L)
        log_dt = jax.random.uniform(ks[2], (H,), dtype=jnp.float32) * (math.log(DT_MAX) - math.log(DT_MIN)) + math.log(DT_MIN)
        C = jax.random.normal(ks[3], (H, N, 2), dtype=jnp.float32)
        log_A_real = jnp.log(0.5 * jnp.ones((H, N), dtype=jnp.float32))
        A_imag = math.pi * jnp.broadcast_to(jnp.arange(N, dtype=jnp.float32), (H, N))
        D = jax.random.normal(ks[4], (H,), dtype=jnp.float32)
        return {'u': u, 'length': length, 'log_dt': log_dt, 'C': C, 'log_A_real': log_A_real, 'A_imag': A_imag, 'D': D}
    _L0_cond_all = _L0_cond_setup()
    _L0_cond_in = {k: v for k, v in _L0_cond_all.items() if k in ('log_dt', 'C', 'log_A_real', 'A_imag', 'D')}
    del _L0_cond_all

    def _L0_ffn_setup():
        import jax, jax.numpy as jnp
        import numpy as np
        HIDDEN = 1024
        INTER = 2752
        GROUPSIZE = 128
        PACK = 8

        def dequant_gptq(qweight, scales, zeros, groupsize):
            K = qweight.shape[0] * PACK
            N = qweight.shape[1]
            k = jnp.arange(K)
            q = qweight[k // PACK, :] >> (k % PACK * 4)[:, None] & 15
            n = jnp.arange(N)
            z = zeros[:, n // PACK] >> (n % PACK * 4)[None, :] & 15
            s = scales.astype(jnp.float32)
            zp = (z.astype(jnp.float32) + 1.0) * s
            g = k // groupsize
            return q.astype(jnp.float32) * s[g] - zp[g]
        key = jax.random.key(seed)
        ks = jax.random.split(key, 11)
        imax = 2147483647
        G_h = HIDDEN // GROUPSIZE
        G_i = (INTER + GROUPSIZE - 1) // GROUPSIZE
        x = (jax.random.normal(ks[0], (2, 512, HIDDEN), dtype=jnp.float32) * 0.5).astype(jnp.float16)
        return {'x': x, 'gate_qweight': jax.random.randint(ks[1], (HIDDEN // PACK, INTER), 0, imax, dtype=jnp.int32), 'gate_scales': (jax.random.uniform(ks[2], (G_h, INTER), dtype=jnp.float32) * 0.01 + 0.001).astype(jnp.float16), 'gate_zeros': jax.random.randint(ks[3], (G_h, INTER // PACK), 0, imax, dtype=jnp.int32), 'up_qweight': jax.random.randint(ks[4], (HIDDEN // PACK, INTER), 0, imax, dtype=jnp.int32), 'up_scales': (jax.random.uniform(ks[5], (G_h, INTER), dtype=jnp.float32) * 0.01 + 0.001).astype(jnp.float16), 'up_zeros': jax.random.randint(ks[6], (G_h, INTER // PACK), 0, imax, dtype=jnp.int32), 'down_qweight': jax.random.randint(ks[7], (INTER // PACK, HIDDEN), 0, imax, dtype=jnp.int32), 'down_scales': (jax.random.uniform(ks[8], (G_i, HIDDEN), dtype=jnp.float32) * 0.01 + 0.001).astype(jnp.float16), 'down_zeros': jax.random.randint(ks[9], (G_i, HIDDEN // PACK), 0, imax, dtype=jnp.int32)}
    _L0_ffn_all = _L0_ffn_setup()
    _L0_ffn_in = {k: v for k, v in _L0_ffn_all.items() if k in ('gate_qweight', 'gate_scales', 'gate_zeros', 'up_qweight', 'up_scales', 'up_zeros', 'down_qweight', 'down_scales', 'down_zeros')}
    del _L0_ffn_all
    return {'x': x, 'itok_B_8_3872': itok_B_8_3872, 'L0_cond_log_dt': _L0_cond_in['log_dt'], 'L0_cond_C': _L0_cond_in['C'], 'L0_cond_log_A_real': _L0_cond_in['log_A_real'], 'L0_cond_A_imag': _L0_cond_in['A_imag'], 'L0_cond_D': _L0_cond_in['D'], 'L0_ffn_gate_qweight': _L0_ffn_in['gate_qweight'], 'L0_ffn_gate_scales': _L0_ffn_in['gate_scales'], 'L0_ffn_gate_zeros': _L0_ffn_in['gate_zeros'], 'L0_ffn_up_qweight': _L0_ffn_in['up_qweight'], 'L0_ffn_up_scales': _L0_ffn_in['up_scales'], 'L0_ffn_up_zeros': _L0_ffn_in['up_zeros'], 'L0_ffn_down_qweight': _L0_ffn_in['down_qweight'], 'L0_ffn_down_scales': _L0_ffn_in['down_scales'], 'L0_ffn_down_zeros': _L0_ffn_in['down_zeros']}

def reference(x, itok_B_8_3872, L0_cond_log_dt, L0_cond_C, L0_cond_log_A_real, L0_cond_A_imag, L0_cond_D, L0_ffn_gate_qweight, L0_ffn_gate_scales, L0_ffn_gate_zeros, L0_ffn_up_qweight, L0_ffn_up_scales, L0_ffn_up_zeros, L0_ffn_down_qweight, L0_ffn_down_scales, L0_ffn_down_zeros):
    import jax
    import jax.numpy as jnp

    def _L0_cond_ref(u, length, log_dt, C, log_A_real, A_imag, D):
        import math
        import jax, jax.numpy as jnp
        import numpy as np
        H, N, B, L = (64, 64, 16, 1024)
        DT_MIN, DT_MAX = (0.001, 0.1)

        def _get_kernel(log_dt, C, log_A_real, A_imag, length):
            Cc = C[..., 0] + 1j * C[..., 1]
            dt = jnp.exp(log_dt)
            A = -jnp.exp(log_A_real) + 1j * A_imag
            dtA = A * dt[:, None]
            P = dtA[:, :, None] * jnp.arange(length, dtype=jnp.float32)
            Cs = Cc * (jnp.exp(dtA) - 1.0) / A
            K = 2.0 * jnp.einsum('hn,hnl->hl', Cs, jnp.exp(P)).real
            return K
        Bq, Hq, Lq = u.shape
        mask = (jnp.arange(Lq) < length[:, None]).astype(u.dtype)
        u_m = u * mask[:, None, :]
        kernel = _get_kernel(log_dt, C, log_A_real, A_imag, Lq)
        n = 2 * Lq
        k_f = jnp.fft.rfft(kernel, n=n)
        u_f = jnp.fft.rfft(u_m, n=n)
        y = jnp.fft.irfft(u_f * k_f, n=n)[..., :Lq]
        y = y + u_m * D[:, None]
        return y * mask[:, None, :]

    def _L0_ffn_ref(x, gate_qweight, gate_scales, gate_zeros, up_qweight, up_scales, up_zeros, down_qweight, down_scales, down_zeros):
        import jax, jax.numpy as jnp
        import numpy as np
        HIDDEN = 1024
        INTER = 2752
        GROUPSIZE = 128
        PACK = 8

        def dequant_gptq(qweight, scales, zeros, groupsize):
            K = qweight.shape[0] * PACK
            N = qweight.shape[1]
            k = jnp.arange(K)
            q = qweight[k // PACK, :] >> (k % PACK * 4)[:, None] & 15
            n = jnp.arange(N)
            z = zeros[:, n // PACK] >> (n % PACK * 4)[None, :] & 15
            s = scales.astype(jnp.float32)
            zp = (z.astype(jnp.float32) + 1.0) * s
            g = k // groupsize
            return q.astype(jnp.float32) * s[g] - zp[g]
        B, S, H = x.shape
        x2 = x.reshape(-1, H).astype(jnp.float32)
        Wg = dequant_gptq(gate_qweight, gate_scales, gate_zeros, GROUPSIZE)
        Wu = dequant_gptq(up_qweight, up_scales, up_zeros, GROUPSIZE)
        Wd = dequant_gptq(down_qweight, down_scales, down_zeros, GROUPSIZE)
        gate = x2 @ Wg
        up = x2 @ Wu
        inter = gate * jax.nn.sigmoid(gate) * up
        out = (inter @ Wd).astype(jnp.float16)
        return out.reshape(B, S, H)
    x = x + _L0_ffn_ref(_L0_cond_ref(x, itok_B_8_3872, L0_cond_log_dt, L0_cond_C, L0_cond_log_A_real, L0_cond_A_imag, L0_cond_D), L0_ffn_gate_qweight, L0_ffn_gate_scales, L0_ffn_gate_zeros, L0_ffn_up_qweight, L0_ffn_up_scales, L0_ffn_up_zeros, L0_ffn_down_qweight, L0_ffn_down_scales, L0_ffn_down_zeros)
    return x

_drawn_inputs = setup_inputs


def setup_inputs(seed=0):
    import zlib

    import numpy as np

    out = dict(_drawn_inputs(seed))
    spreads = {'L0_cond_log_A_real': (-0.6931471824645996, 0.2)}
    factors = {}
    for name, (base, spread) in spreads.items():
        noise = np.random.default_rng([zlib.crc32(name.encode()), seed]).standard_normal(out[name].shape)
        drawn = base * np.exp(spread * noise) if base else spread * noise
        out[name] = jnp.asarray(drawn.astype(out[name].dtype))
    for name, factor in factors.items():
        out[name] = (out[name] * factor).astype(out[name].dtype)
    return out
```

```python
from contextlib import ExitStack

import numpy as np

import concourse.bass as bass
from concourse import mybir

F32 = mybir.dt.float32
F32R = mybir.dt.float32r
F16 = mybir.dt.float16
BF16 = mybir.dt.bfloat16
I32 = mybir.dt.int32
U16 = mybir.dt.uint16
ALU = mybir.AluOpType
ACT = mybir.ActivationFunctionType

P = 128
B, H, L = 32, 64, 1024
NS = 64
HID, INTER, PACK, GROUP = 1024, 2752, 8, 128
KT = L // P
HG = 4
NG = H // HG
HC = 16
NHC = H // HC
CONV_STEPS = 21
FFN_STEPS = 124
TOK = B * H
HALF = TOK // 2
NC = 11
NT = 8
LAST = INTER - NT * 256 - 2 * 256 - P
KPAD = P + L
TRING = 8

MAGIC = float(1.5 * 2 ** 23)
TWO_PI = 2 * np.pi
PI1 = 6.28125
PI2 = float(np.float32(int((TWO_PI - PI1) * 2 ** 21) / 2 ** 21))
PI3 = float(np.float32(TWO_PI - PI1 - PI2))
LN2 = float(np.log(2))
LN2_1 = 0.693359375
LN2_2 = float(np.float32(LN2 - LN2_1))
PI_BELOW = float(np.nextafter(np.float32(np.pi), np.float32(0)))

C_B, C_A, C_LCOL = 0, 32, 64
C_OFFR, C_OFFR_T, C_OFFL, C_OFFL_T, C_NHPI, C_OFFC, C_OFFC_T = 72, 73, 74, 75, 76, 77, 78
C_N = 80


def const_table():
    t = np.zeros((P, C_N), np.float32)
    t[:, C_B:C_B + 32] = np.arange(32)
    t[:, C_A:C_A + 32] = 32 * np.arange(32)
    t[:, C_LCOL:C_LCOL + KT] = P * np.arange(KT)[None, :] + np.arange(P)[:, None]
    real = np.arange(P) < NS
    t[:, C_OFFR] = np.where(real, np.pi / 2, 0)
    t[:, C_OFFR_T] = np.where(real, 0.25, 0)
    t[:, C_OFFL] = np.where(real, np.pi / 2, np.pi)
    t[:, C_OFFL_T] = np.where(real, 0.25, 0.5)
    t[:, C_NHPI] = -np.pi / 2
    t[:, C_OFFC] = np.pi / 2
    t[:, C_OFFC_T] = 0.25
    return t


def shift_table():
    t = np.zeros((P, 2 * NC), np.int32)
    for c in range(NC):
        for e in range(2):
            t[:, 2 * c + e] = 4 * (c % 4 + 4 * e) if c < NT else 4 * (np.arange(P) % 8)
    return t


class Count:

    def __init__(self, sem, start=0):
        self.sem, self.base, self.n, self.sealed = sem, 0, start, None

    def inc(self, ins, by=1):
        ins.then_inc(self.sem, by)
        self.n += by

    def value(self):
        return self.base + self.n if not isinstance(self.base, int) or self.base else self.n

    def enter(self, i, per):
        self.saved = (self.base, self.n, per)
        self.base = self.base + i * per

    def leave(self, times):
        base, n, per = self.saved
        assert self.n - n == per, (self.n - n, per)
        self.base, self.n = base, n + times * per


def build_program(nc, x, itok, log_dt, C, log_A, A_imag, D, gq, gs, gz, uq, us, uz, dq, ds, dz,
                  ctab, stab, ident_in, out):
    kpad = nc.dram_tensor("kernel_padded", (H, KPAD), F32, kind="Internal").ap()
    ysc = nc.dram_tensor("y_scratch", (L, TOK), F32, kind="Internal").ap()
    with ExitStack() as whole:
        def psum(i):
            return whole.enter_context(nc.psum_tensor(f"bank{i}", [P, 512], F32))

        bank = [psum(i) for i in range(8)]
        conv_stage(nc, bank, kpad, ysc, x, itok, log_dt, C, log_A, A_imag, D, ctab, ident_in)
        ffn_stage(nc, bank, ysc, x, gq, gs, gz, uq, us, uz, dq, ds, dz, stab, out)


def conv_stage(nc, bank, kpad, ysc, x, itok, log_dt, C, log_A, A_imag, D, ctab, ident_in):
    with ExitStack() as ctx:
        def sb(name, shape, dt=F32):
            return ctx.enter_context(nc.sbuf_tensor(name, shape, dt))

        def sem(name):
            return ctx.enter_context(nc.semaphore(name))

        tab = sb("tab", [P, C_N])
        ident = sb("ident", [P, P])
        iota_l = sb("iota_l", [P, L])
        len_i = sb("len_i", [P, 1], I32)
        len_col = sb("len_col", [P, 1])
        lens_i = sb("lens_i", [P, B], I32)
        lens = sb("lens", [P, B])
        mask_t = sb("mask_t", [P, KT, B])
        logs = sb("logs", [H, 1 + NS])
        exps = sb("exps", [H, 1 + NS])
        power = sb("power", [H, 1 + NS])
        power_i = sb("power_i", [H, 1 + NS], I32)
        rest = sb("rest", [H, 1 + NS])
        c_in = sb("c_in", [H, NS, 2])
        ai_in = sb("ai_in", [H, NS])
        d_row = sb("d_row", [1, H])
        dt, eA = exps[:, 0:1], exps[:, 1:1 + NS]
        (are, are_arg, aim, exp_are, half, arg_s, arg_c, sn, cs, em1, t1, t2, t3, zr, zi, inv) = (
            sb(n, [H, NS]) for n in ("are", "are_arg", "aim", "exp_are", "half", "arg_s", "arg_c", "sn",
                                     "cs", "em1", "t1", "t2", "t3", "zr", "zi", "inv"))
        par_h = sb("par_h", [H, 4, 2, NS])
        par = sb("par", [P, 4, H])
        (e_r, e_l, th_r, th_l, turns, s_r, p_1, p_2, left, right) = (
            sb(n, [P, HC, 32]) for n in ("e_r", "e_l", "th_r", "th_l", "turns", "s_r", "p_1", "p_2", "left",
                                         "right"))
        k_sb = sb("k_sb", [32, HC, 32])
        zero = sb("zero", [H, P])
        toep = sb("toep", [P, TRING, L])
        x_in = sb("x_in", [P, 2, L])
        x_rev = sb("x_rev", [P, 2, L])
        u_t = sb("u_t", [P, 2, KT, P])
        y_nat = sb("y_nat", [P, 2, KT, P])

        par_in, tab_in, len_in = sem("par_in"), sem("tab_in"), sem("len_in")
        x_loaded = [sem("x_loaded0"), sem("x_loaded1")]
        t_loaded = [sem(f"t_loaded{i}") for i in range(TRING)]
        y_stored = [sem("y_stored0"), sem("y_stored1")]
        k_stored, zero_stored, const_ready = sem("k_stored"), sem("zero_stored"), sem("const_ready")
        dve_step = sem("dve_step")
        f_args, f_done = sem("f_args"), sem("f_done")
        par_ready, par_turned = sem("par_ready"), sem("par_turned")
        lr_ready, k_mm, k_sb_ready = sem("lr_ready"), sem("k_mm"), sem("k_sb_ready")
        rev_ready, u_turned, u_ready = sem("rev_ready"), sem("u_turned"), sem("u_ready")
        conv_mm, y_ready = sem("conv_mm"), sem("y_ready")

        turn_ps = [bank[0], bank[1]]
        conv_ps = [bank[2:4], bank[4:6]]
        k_ps, par_ps = bank[6], bank[7]

        block = ctx.enter_context(nc.Block())

        def x_rows(g):
            return bass.AP(x.tensor, g * (HG * L), [[L, HG], [H * L, B], [1, L]])

        @block.sync
        def _(sp):
            for y in y_stored:
                sp.sem_inc(y, 16)
            sp.dma_start(logs[:, 0:1], log_dt.rearrange("(h o) -> h o", o=1)).then_inc(par_in, 16)
            sp.dma_start(logs[:, 1:1 + NS], log_A).then_inc(par_in, 16)
            sp.dma_start(ai_in[:], A_imag).then_inc(par_in, 16)
            sp.dma_start(c_in[:], C).then_inc(par_in, 16)
            sp.dma_start(d_row[:], D.rearrange("(o h) -> o h", o=1)).then_inc(par_in, 16)
            sp.dma_start(tab[:], ctab).then_inc(tab_in, 16)
            sp.dma_start(ident[:], ident_in).then_inc(tab_in, 16)
            for hh in range(HG):
                sp.dma_start(len_i[B * hh:B * hh + B, :], itok.rearrange("(b o) -> b o", o=1)).then_inc(len_in, 16)
            sp.dma_start(lens_i[:], bass.AP(itok.tensor, 0, [[0, P], [1, B]])).then_inc(len_in, 16)
            for g in range(2):
                sp.dma_start(x_in[:, g, :], x_rows(g)).then_inc(x_loaded[g], 16)
            sp.wait_ge(zero_stored, 16)

            def load_toeplitz(g, half_):
                for hh in range(HG):
                    slot = HG * half_ + hh
                    sp.wait_ge(conv_mm, g * HG + (hh + 1))
                    src = bass.AP(kpad.tensor, (g * HG + hh) * KPAD + 1, [[1, P], [1, L]])
                    sp.dma_start(toep[:, slot, :], src).then_inc(t_loaded[slot], 16)

            def piece(hc, last):
                for q in range(4):
                    g = hc * 4 + q
                    if not (last and q >= 2):
                        sp.wait_ge(rev_ready, g + 1)
                        sp.dma_start(x_in[:, q % 2, :], x_rows(g + 2)).then_inc(x_loaded[q % 2], 16)
                    sp.wait_ge(y_ready, g * 2 + 6)
                    dst = bass.AP(ysc.tensor, g * P, [[TOK, P], [P * TOK, KT], [1, P]])
                    sp.dma_start(dst, y_nat[:, q % 2, :, :]).then_inc(y_stored[q % 2], 16)
                    if q == 2 and not last:
                        sp.wait_ge(k_stored, hc * 16 + 32)
                    if not (last and q >= 2):
                        load_toeplitz(g + 2, q % 2)

            sp.wait_ge(k_stored, 16)
            load_toeplitz(0, 0)
            load_toeplitz(1, 1)
            with sp.Fori(0, NHC - 1) as hc:
                piece(hc, False)
            piece(NHC - 1, True)
            for y in y_stored:
                sp.wait_ge(y, 16 + 16 * NG // 2)

        @block.gpsimd
        def _(pool):
            pool.iota(iota_l[:], [[1, L]], base=0, channel_multiplier=0,
                      allow_small_or_imprecise_dtypes=True).then_inc(const_ready, 1)
            pool.memset(zero[:], 0.0).then_inc(const_ready, 1)
            pool.wait_ge(const_ready, 2)
            pool.dma_start(kpad[:, 0:P], zero[:]).then_inc(zero_stored, 16)
            with pool.Fori(0, NHC) as hc:
                pool.wait_ge(k_sb_ready, hc + 2)
                dst = bass.AP(kpad.tensor, hc * (HC * KPAD) + P, [[32, 32], [KPAD, HC], [1, 32]])
                pool.dma_start(dst, k_sb[:]).then_inc(k_stored, 16)
                pool.wait_ge(k_stored, hc * 16 + 16)

        @block.scalar
        def _(act):
            act.sem_inc(u_ready, 2)
            act.wait_ge(f_args, 1)
            act.activation(exp_are[:], are_arg[:], ACT.Exp).then_inc(f_done, 1)
            act.wait_ge(f_args, 2)
            act.activation(sn[:], arg_s[:], ACT.Sin).then_inc(f_done, 1)
            act.wait_ge(f_args, 3)
            act.activation(cs[:], arg_c[:], ACT.Sin).then_inc(f_done, 1)

            def functions_right(hc):
                act.wait_ge(f_args, hc * 5 + 4)
                act.activation(e_r[:], e_r[:], ACT.Exp).then_inc(f_done, 1)
                act.wait_ge(f_args, hc * 5 + 5)
                act.activation(e_l[:], e_l[:], ACT.Exp).then_inc(f_done, 1)
                act.wait_ge(f_args, hc * 5 + 6)
                act.activation(s_r[:], s_r[:], ACT.Sin).then_inc(f_done, 1)

            def functions_left(hc):
                act.wait_ge(f_args, hc * 5 + 7)
                act.activation(p_1[:], p_1[:], ACT.Sin).then_inc(f_done, 1)
                act.wait_ge(f_args, hc * 5 + 8)
                act.activation(p_2[:], p_2[:], ACT.Sin, bias=tab[:, C_NHPI:C_NHPI + 1]).then_inc(f_done, 1)

            def take_turned(g, half_):
                act.wait_ge(u_turned, g + 3)
                act.wait_ge(conv_mm, g * HG + 4)
                for k in range(2):
                    act.copy(u_t[:, half_, 4 * k:4 * k + 4, :],
                             turn_ps[k][:].rearrange("p (c r) -> p c r", c=4)).then_inc(u_ready, 1)

            def piece(hc, last):
                for q in range(4):
                    g = hc * 4 + q
                    if not (last and q == 3):
                        take_turned(g + 1, (q + 1) % 2)
                    if not last and q == 0:
                        functions_right(hc + 1)
                    if not last and q == 1:
                        functions_left(hc + 1)

            act.wait_ge(tab_in, 32)
            functions_right(0)
            functions_left(0)
            take_turned(0, 0)
            with act.Fori(0, NHC - 1) as hc:
                piece(hc, False)
            piece(NHC - 1, True)

        @block.vector
        def _(dve):
            step = Count(dve_step)

            def do(ins):
                step.inc(ins)
                dve.wait_ge(dve_step, step.value())

            def col(i):
                return tab[:, i:i + 1]

            dve.sem_inc(lr_ready, 1)
            dve.sem_inc(k_sb_ready, 1)
            dve.sem_inc(y_ready, 4)
            dve.wait_ge(par_in, 80)
            dve.wait_ge(tab_in, 32)

            def series(p, r):
                do(dve.tensor_scalar(p, r, 1 / 5040.0, None, ALU.mult))
                for c in (1 / 720.0, 1 / 120.0, 1 / 24.0, 1 / 6.0, 0.5, 1.0):
                    do(dve.scalar_tensor_tensor(out=p, in0=p, scalar=c, in1=r, op0=ALU.add, op1=ALU.mult))

            do(dve.tensor_scalar(logs[:], logs[:], -87.0, 88.0, ALU.max, ALU.min))
            do(dve.tensor_scalar(power[:], logs[:], 1 / LN2, None, ALU.mult))
            do(dve.tensor_scalar(power[:], power[:], MAGIC, MAGIC, ALU.add, ALU.subtract))
            do(dve.scalar_tensor_tensor(out=rest[:], in0=power[:], scalar=-LN2_1, in1=logs[:], op0=ALU.mult, op1=ALU.add))
            do(dve.scalar_tensor_tensor(out=rest[:], in0=power[:], scalar=-LN2_2, in1=rest[:], op0=ALU.mult, op1=ALU.add))
            series(exps[:], rest[:])
            do(dve.tensor_scalar(power_i[:], power[:], 127.0, None, ALU.add))
            do(dve.tensor_scalar(power_i[:], power_i[:], 23, None, ALU.logical_shift_left))
            do(dve.scalar_tensor_tensor(out=exps[:], in0=exps[:], scalar=1.0, in1=power_i[:].bitcast(F32),
                                        op0=ALU.add, op1=ALU.mult))
            do(dve.tensor_scalar(are[:], eA, dt, -1.0, ALU.mult, ALU.mult))
            dve.tensor_copy(are_arg[:], are[:]).then_inc(f_args, 1)
            do(dve.tensor_scalar(aim[:], ai_in[:], dt, None, ALU.mult))
            do(dve.tensor_scalar(half[:], aim[:], 0.5, None, ALU.mult))
            for arg, quarter in ((arg_s, 0.0), (arg_c, 0.25)):
                do(dve.tensor_scalar(t1[:], half[:], 1 / TWO_PI, quarter, ALU.mult, ALU.add))
                do(dve.tensor_scalar(t1[:], t1[:], MAGIC, MAGIC, ALU.add, ALU.subtract))
                do(dve.scalar_tensor_tensor(out=arg[:], in0=t1[:], scalar=-PI1, in1=half[:], op0=ALU.mult, op1=ALU.add))
                do(dve.scalar_tensor_tensor(out=arg[:], in0=t1[:], scalar=-PI2, in1=arg[:], op0=ALU.mult, op1=ALU.add))
                do(dve.scalar_tensor_tensor(out=arg[:], in0=t1[:], scalar=-PI3, in1=arg[:], op0=ALU.mult, op1=ALU.add))
                do(dve.tensor_scalar(arg[:], arg[:], quarter * TWO_PI, PI_BELOW, ALU.add, ALU.min))
                dve.tensor_scalar(arg[:], arg[:], -PI_BELOW, None, ALU.max).then_inc(f_args, 1)
            do(dve.tensor_scalar(t2[:], are[:], -0.25, 0.25, ALU.max, ALU.min))
            series(em1[:], t2[:])
            dve.wait_ge(f_done, 3)
            do(dve.tensor_scalar(t1[:], exp_are[:], 1.0, None, ALU.subtract))
            do(dve.tensor_tensor(t2[:], t2[:], are[:], ALU.is_equal))
            do(dve.tensor_tensor(em1[:], em1[:], t2[:], ALU.mult))
            do(dve.tensor_scalar(t2[:], t2[:], -1.0, 1.0, ALU.mult, ALU.add))
            do(dve.tensor_tensor(t1[:], t1[:], t2[:], ALU.mult))
            do(dve.tensor_tensor(em1[:], em1[:], t1[:], ALU.add))
            do(dve.scalar_tensor_tensor(out=t1[:], in0=sn[:], scalar=-2.0, in1=sn[:], op0=ALU.mult, op1=ALU.mult))
            do(dve.scalar_tensor_tensor(out=t2[:], in0=t1[:], scalar=1.0, in1=em1[:], op0=ALU.add, op1=ALU.mult))
            do(dve.tensor_tensor(t1[:], t1[:], t2[:], ALU.add))
            do(dve.scalar_tensor_tensor(out=t2[:], in0=sn[:], scalar=2.0, in1=cs[:], op0=ALU.mult, op1=ALU.mult))
            do(dve.tensor_tensor(t2[:], t2[:], exp_are[:], ALU.mult))
            do(dve.tensor_tensor(inv[:], eA, eA, ALU.mult))
            do(dve.tensor_tensor(t3[:], ai_in[:], ai_in[:], ALU.mult))
            do(dve.tensor_tensor(inv[:], inv[:], t3[:], ALU.add))
            do(dve.reciprocal(inv[:], inv[:]))
            do(dve.tensor_tensor(zr[:], t2[:], ai_in[:], ALU.mult))
            do(dve.tensor_tensor(t3[:], t1[:], eA, ALU.mult))
            do(dve.tensor_tensor(zr[:], zr[:], t3[:], ALU.subtract))
            do(dve.tensor_tensor(zr[:], zr[:], inv[:], ALU.mult))
            do(dve.tensor_tensor(zi[:], t2[:], eA, ALU.mult))
            do(dve.tensor_tensor(t3[:], t1[:], ai_in[:], ALU.mult))
            do(dve.scalar_tensor_tensor(out=zi[:], in0=zi[:], scalar=-1.0, in1=t3[:], op0=ALU.mult, op1=ALU.subtract))
            do(dve.tensor_tensor(zi[:], zi[:], inv[:], ALU.mult))
            cr, ci = c_in[:, :, 0], c_in[:, :, 1]
            do(dve.tensor_tensor(t1[:], cr, zr[:], ALU.mult))
            do(dve.tensor_tensor(t2[:], ci, zi[:], ALU.mult))
            do(dve.tensor_tensor(t1[:], t1[:], t2[:], ALU.subtract))
            do(dve.tensor_tensor(t2[:], cr, zi[:], ALU.mult))
            do(dve.tensor_tensor(t3[:], ci, zr[:], ALU.mult))
            do(dve.tensor_tensor(t2[:], t2[:], t3[:], ALU.add))
            for n in range(2):
                dve.tensor_copy(par_h[:, 0, n, :], are[:]).then_inc(par_ready, 1)
                dve.tensor_copy(par_h[:, 1, n, :], aim[:]).then_inc(par_ready, 1)
                dve.tensor_scalar(par_h[:, 2, n, :], t1[:], 2.0, None, ALU.mult).then_inc(par_ready, 1)
                dve.tensor_scalar(par_h[:, 3, n, :], t2[:], 2.0, None, ALU.mult).then_inc(par_ready, 1)
            dve.wait_ge(par_turned, 1)
            do(dve.tensor_copy(par[:], par_ps[:, 0:4 * H].rearrange("p (v h) -> p v h", v=4)))

            def wide(v, hc):
                return bass.AP(par[:].tensor, hc * HC + v * H, [[4 * H, P], [1, HC], [0, 32]])

            def exponents(c0):
                return bass.AP(tab[:].tensor, c0, [[C_N, P], [0, HC], [1, 32]])

            def arguments(hc):
                dve.wait_ge(lr_ready, hc + 1)
                dve.tensor_tensor(e_r[:], wide(0, hc), exponents(C_B), ALU.mult).then_inc(f_args, 1)
                dve.tensor_tensor(e_l[:], wide(0, hc), exponents(C_A), ALU.mult).then_inc(f_args, 1)
                dve.tensor_tensor(th_r[:], wide(1, hc), exponents(C_B), ALU.mult)
                do(dve.tensor_tensor(th_l[:], wide(1, hc), exponents(C_A), ALU.mult))

            def reduce(arg, th, off, off_t):
                do(dve.tensor_scalar(turns[:], th[:], 1 / TWO_PI, None, ALU.mult))
                do(dve.tensor_scalar(turns[:], turns[:], col(off_t), None, ALU.add))
                do(dve.tensor_scalar(turns[:], turns[:], MAGIC, MAGIC, ALU.add, ALU.subtract))
                do(dve.scalar_tensor_tensor(out=arg[:], in0=turns[:], scalar=-PI1, in1=th[:], op0=ALU.mult, op1=ALU.add))
                do(dve.scalar_tensor_tensor(out=arg[:], in0=turns[:], scalar=-PI2, in1=arg[:], op0=ALU.mult, op1=ALU.add))
                do(dve.scalar_tensor_tensor(out=arg[:], in0=turns[:], scalar=-PI3, in1=arg[:], op0=ALU.mult, op1=ALU.add))
                do(dve.tensor_scalar(arg[:], arg[:], col(off), None, ALU.add))

            def reduce_right():
                reduce(s_r, th_r, C_OFFR, C_OFFR_T)
                dve.tensor_scalar(s_r[:], s_r[:], -PI_BELOW, PI_BELOW, ALU.max, ALU.min).then_inc(f_args, 1)

            def reduce_left():
                reduce(p_1, th_l, C_OFFL, C_OFFL_T)
                do(dve.tensor_scalar(p_1[:], p_1[:], -PI_BELOW, PI_BELOW, ALU.max, ALU.min))
                do(dve.scalar_tensor_tensor(out=p_2[:], in0=p_1[:], scalar=-1.0, in1=p_1[:], op0=ALU.mult, op1=ALU.max))
                dve.sem_inc(f_args, 2)

            def combine(hc):
                dve.wait_ge(f_done, hc * 5 + 8)
                dve.wait_ge(k_mm, hc + 1)
                dve.tensor_tensor(right[:], e_r[:], s_r[:], ALU.mult)
                do(dve.tensor_tensor(p_1[:], p_1[:], wide(2, hc), ALU.mult))
                do(dve.tensor_tensor(p_2[:], p_2[:], wide(3, hc), ALU.mult))
                do(dve.tensor_tensor(p_1[:], p_1[:], p_2[:], ALU.subtract))
                dve.tensor_tensor(left[:], p_1[:], e_l[:], ALU.mult).then_inc(lr_ready, 1)

            def take_kernel(hc):
                dve.wait_ge(k_mm, hc + 2)
                if not (isinstance(hc, int) and hc == 0):
                    dve.wait_ge(k_stored, hc * 16)
                do(dve.tensor_copy(k_sb[:], k_ps[0:32, :].rearrange("p (h b) -> p h b", h=HC)))
                d_piece = bass.AP(d_row[:].tensor, hc * HC, [[H, 1], [1, HC], [1, 1]])
                dve.tensor_tensor(k_sb[0:1, :, 0:1], k_sb[0:1, :, 0:1], d_piece, ALU.add).then_inc(k_sb_ready, 1)

            def mask_and_reverse(g, half_):
                dve.wait_ge(x_loaded[half_], (g - half_) * 8 + 16)
                dve.wait_ge(u_turned, g + 1)
                dve.scalar_tensor_tensor(
                    out=x_rev[:, half_, :].rearrange("p (c l) -> p c l", c=KT)[:, :, ::-1],
                    in0=iota_l[:].rearrange("p (c l) -> p c l", c=KT), scalar=len_col[:, 0:1],
                    in1=x_in[:, half_, :].rearrange("p (c l) -> p c l", c=KT),
                    op0=ALU.is_lt, op1=ALU.mult).then_inc(rev_ready, 1)

            def take_conv(g, half_):
                dve.wait_ge(y_stored[half_], (g - half_) * 8 + 16)
                for k in range(2):
                    dve.wait_ge(conv_mm, g * HG + (TRING + 2 * k + 2))
                    dve.tensor_tensor(
                        y_nat[:, half_, :, 64 * k:64 * k + 64].rearrange("p c (h b) -> p h c b", h=2),
                        conv_ps[half_][k][:].rearrange("p (h c b) -> p h c b", h=2, c=KT),
                        bass.AP(mask_t[:].tensor, 0, [[KT * B, P], [0, 2], [B, KT], [1, B]]),
                        ALU.mult).then_inc(y_ready, 1)

            arguments(0)
            reduce_right()
            reduce_left()
            dve.wait_ge(len_in, 80)
            do(dve.tensor_copy(len_col[:], len_i[:]))
            do(dve.tensor_copy(lens[:], lens_i[:]))
            for c in range(KT):
                dve.tensor_scalar(mask_t[:, c, :], lens[:], col(C_LCOL + c), None, ALU.is_gt)
            dve.wait_ge(const_ready, 1)
            mask_and_reverse(0, 0)
            mask_and_reverse(1, 1)
            combine(0)
            take_kernel(0)

            def piece(hc, last):
                for q in range(4):
                    g = hc * 4 + q
                    if q == 0 and not last:
                        arguments(hc + 1)
                        reduce_right()
                    if q == 1 and not last:
                        reduce_left()
                    if q == 2 and not last:
                        combine(hc + 1)
                    if q == 3 and not last:
                        take_kernel(hc + 1)
                    if not (last and q >= 2):
                        mask_and_reverse(g + 2, q % 2)
                    take_conv(g, q % 2)

            with dve.Fori(0, NHC - 1) as hc:
                step.enter(hc, CONV_STEPS)
                piece(hc, False)
                step.leave(NHC - 1)
            piece(NHC - 1, True)

        @block.tensor
        def _(pe):
            pe.sem_inc(k_mm, 1)
            pe.sem_inc(u_turned, 2)
            pe.sem_inc(conv_mm, TRING)
            pe.wait_ge(tab_in, 32)
            pe.wait_ge(par_ready, 8)
            for v in range(4):
                mm = pe.transpose(par_ps[:, v * H:(v + 1) * H], par_h[:, v, :, :].rearrange("p n s -> p (n s)"),
                                  ident[0:H, 0:H])
            mm.then_inc(par_turned, 1)

            def turn(g, half_):
                pe.wait_ge(rev_ready, g + 1)
                pe.wait_ge(u_ready, g * 2 + 2)
                for c in range(KT):
                    mm = pe.transpose(turn_ps[c // 4][:, P * (c % 4):P * (c % 4) + P],
                                      x_rev[:, half_, P * c:P * c + P], ident[:])
                mm.then_inc(u_turned, 1)

            def multiply_kernel(hc):
                pe.wait_ge(lr_ready, hc + 2)
                pe.wait_ge(k_sb_ready, hc + 1)
                for h in range(HC):
                    mm = pe.matmul(k_ps[0:32, 32 * h:32 * h + 32], left[:, h, :], right[:, h, :],
                                   start=True, stop=True)
                mm.then_inc(k_mm, 1)

            def convolve(hc, q):
                g, half_ = hc * 4 + q, q % 2
                pe.wait_ge(u_ready, g * 2 + 4)
                for hh in range(HG):
                    n = HG * q + hh
                    slot, k = n % TRING, hh // 2
                    pe.wait_ge(t_loaded[slot], hc * (16 * HC // TRING) + 16 * (n // TRING + 1))
                    if hh % 2 == 0:
                        pe.wait_ge(y_ready, g * 2 + (k + 1))
                    base = 256 * (hh % 2)
                    for d in range(KT):
                        mm = pe.matmul(
                            conv_ps[half_][k][:, base + B * d:base + 256],
                            toep[:, slot, P * d:P * d + P],
                            u_t[:, half_, 0:KT - d, B * hh:B * hh + B],
                            start=(d == 0), stop=(d == KT - 1))
                    mm.then_inc(conv_mm, 1)

            multiply_kernel(0)
            turn(0, 0)

            def piece(hc, last):
                for q in range(4):
                    if not (last and q == 3):
                        turn(hc * 4 + (q + 1), (q + 1) % 2)
                    convolve(hc, q)
                    if q == 2 and not last:
                        multiply_kernel(hc + 1)

            with pe.Fori(0, NHC - 1) as hc:
                piece(hc, False)
            piece(NHC - 1, True)


def ffn_stage(nc, bank, ysc, x, gq, gs, gz, uq, us, uz, dq, ds, dz, stab, out):
    with ExitStack() as ctx:
        def sb(name, shape, dt=F32):
            return ctx.enter_context(nc.sbuf_tensor(name, shape, dt))

        def sem(name):
            return ctx.enter_context(nc.semaphore(name))

        y_h = sb("y_h", [P, KT, HALF], F32R)
        y_l = sb("y_l", [P, KT, HALF], F32R)
        w_h = {m: sb(f"w{m}_h", [P, KT * P], F32R) for m in ("g", "u", "d0", "d1")}
        w_l = {m: sb(f"w{m}_l", [P, KT * P], F32R) for m in ("g", "u", "d0", "d1")}
        mid_h = sb("mid_h", [P, 2, HALF], F32R)
        mid_l = sb("mid_l", [P, 2, HALF], F32R)
        acc = sb("acc", [P, HALF // P, HID])
        w_full = sb("w_full", [P, 2, KT * P])
        silu = sb("silu", [P, 2, 512])
        mid = sb("mid", [P, 2, 512])
        q_in = {m: sb(f"q{m}_in", [P, 1024], I32) for m in ("g", "u")}
        s_in = {m: sb(f"s{m}_in", [P, 1024], F16) for m in ("g", "u")}
        z_in = {m: sb(f"z{m}_in", [P, 128], I32) for m in ("g", "u")}
        qd_in = [sb(f"qd_in{e}", [P, HID], I32) for e in range(2)]
        sd_in = [sb(f"sd_in{e}", [P, HID], F16) for e in range(2)]
        zd_in = [sb(f"zd_in{e}", [P, HID // PACK], I32) for e in range(2)]
        shifts = sb("shifts", [P, 2 * NC], I32)
        z_one = {m: sb(f"z{m}_one", [P, 1024], BF16) for m in ("g", "u", "d")}
        diff = {m: sb(f"diff_{m}", [P, KT * P], BF16) for m in ("g", "u", "d0", "d1")}
        s_tile = {m: sb(f"s_tile_{m}", [P, P], F16) for m in ("g", "u")}
        x_fin = w_full
        ffn16 = sb("ffn16", [P, HID], F16)

        shifts_in = sem("shifts_in")
        y_loaded = [sem(f"y_loaded{k}") for k in range(KT)]
        y_cast, y_ready2 = sem("y_cast"), sem("y_ready2")
        gu_in = {m: sem(f"{m}_in") for m in ("g", "u")}
        gu_used = {m: sem(f"{m}_used") for m in ("g", "u")}
        d_in = [sem(f"d_in{e}") for e in range(2)]
        x_fin_in = [sem("x_fin_in0"), sem("x_fin_in1")]
        out_ready, out_stored = sem("out_ready"), sem("out_stored")
        step2 = sem("step2")
        diff_ready, full_ready, high_ready, slot_ready = (
            sem("diff_ready"), sem("full_ready"), sem("high_ready"), sem("slot_ready"))
        g_mm, u_mm, d_mm = sem("g_mm"), sem("u_mm"), sem("d_mm")
        silu_done, mid_done, mid_cast, mid_ready, acc_done = (
            sem("silu_done"), sem("mid_done"), sem("mid_cast"), sem("mid_ready"), sem("acc_done"))

        g_ps, u_ps, d_ps = bank[0:2], bank[2:4], bank[4:8]

        ORDER = ["g", "d0", "d1", "u", "g", "u"]

        block = ctx.enter_context(nc.Block())
        NLOAD = 3

        @block.sync
        def _(sp):
            src = {"g": (gq, gs, gz), "u": (uq, us, uz)}

            def load_gu(m, n0, width, number):
                q, s, z = src[m]
                sp.wait_ge(gu_used[m], number + 1)
                sp.dma_start(q_in[m][:, 0:width], q[:, n0:n0 + width]).then_inc(gu_in[m], 16)
                sp.dma_start(s_in[m][:, 0:width],
                             bass.AP(s.tensor, n0, [[INTER, 8], [0, 16], [1, width]])).then_inc(gu_in[m], 16)
                sp.dma_start(z_in[m][:, 0:width // PACK],
                             bass.AP(z.tensor, n0 // PACK, [[INTER // PACK, 8], [0, 16], [1, width // PACK]])
                             ).then_inc(gu_in[m], 16)

            def load_down(c, e, number):
                sp.wait_ge(full_ready, number * 6 + (4 + e))
                if c < NT:
                    t, n, G = c // 4, P, HID // PACK
                    q_src = dq[P * t:P * t + P, :]
                    s_src = bass.AP(ds.tensor, 8 * t * HID, [[HID, 8], [0, 16], [1, HID]])
                    z_src = bass.AP(dz.tensor, 8 * t * G, [[G, 8], [0, 16], [1, G]])
                else:
                    v = 2 * (c - NT) + e
                    n, G = (P if 2 * c + e < 2 * NC - 1 else LAST), HID // PACK
                    q_src = bass.AP(dq.tensor, (256 + 16 * v) * HID, [[HID, n // 8], [0, 8], [1, HID]])
                    s_src = bass.AP(ds.tensor, (16 + v) * HID, [[0, n], [1, HID]])
                    z_src = bass.AP(dz.tensor, (16 + v) * G, [[0, n], [1, G]])
                sp.dma_start(qd_in[e][0:n, :], q_src).then_inc(d_in[e], 16)
                sp.dma_start(sd_in[e][0:n, :], s_src).then_inc(d_in[e], 16)
                sp.dma_start(zd_in[e][0:n, :], z_src).then_inc(d_in[e], 16)

            sp.dma_start(shifts[:], stab).then_inc(shifts_in, 16)
            load_gu("g", 0, 1024, 0)
            load_gu("u", 0, 1024, 0)
            for e in range(2):
                load_down(0, e, 0)
            with sp.Fori(0, 2) as hf:
                for c in range(NC):
                    for e in range(2):
                        load_down((c + 1) % NC, e, hf * NC + (c + 1))
                    if c in (3, 7, NC - 1):
                        n0, width = {3: (1024, 1024), 7: (2048, INTER - 2048), NC - 1: (0, 1024)}[c]
                        number = {3: 1, 7: 2, NC - 1: 3}[c]
                        for m in ("g", "u"):
                            load_gu(m, n0, width, hf * NLOAD + number)
                def rows(t, n):
                    return bass.AP(t.tensor, hf * (H // 2 * L) + n * (HG * L), [[L, HG], [H * L, B], [1, L]])

                sp.wait_ge(slot_ready, (hf + 1) * (6 * NC) + 4)
                for tt in range(2):
                    sp.dma_start(x_fin[:, tt, :], rows(x, tt)).then_inc(x_fin_in[tt], 16)
                for tt in range(HALF // P):
                    sp.wait_ge(out_ready, hf * (HALF // P) + (tt + 1))
                    sp.dma_start(rows(out, tt), acc[:, tt, :]).then_inc(out_stored, 16)
                    if tt + 2 < HALF // P:
                        sp.dma_start(x_fin[:, tt % 2, :], rows(x, tt + 2)).then_inc(x_fin_in[tt % 2], 16)
            sp.wait_ge(out_stored, 16 + 16 * 2 * (HALF // P))
            for e in range(2):
                sp.wait_ge(d_in[e], 48 * (2 * NC + 1))
            for m in ("g", "u"):
                sp.wait_ge(gu_in[m], 48 * (2 * NLOAD + 1))

        @block.vector
        def _(dve):
            step = Count(step2)

            def do(ins):
                step.inc(ins)
                dve.wait_ge(step2, step.value())

            for m in ("g", "u"):
                dve.sem_inc(gu_used[m], 1)
            dve.sem_inc(mid_done, 1)
            dve.sem_inc(acc_done, 4)

            def nibbles(dst, src_, a):
                return dve.tensor_scalar(dst, src_, 4 * a, 15, ALU.logical_shift_right, ALU.bitwise_and)

            def unpack_zeros(z, dst, n, width):
                words = z[0:n, 0:width // PACK].bitcast(U16).rearrange("p (m b) -> p m b", b=2)
                raw = dst[0:n, 0:width].bitcast(U16)
                for a in range(4):
                    ins = nibbles(raw.rearrange("p (m b a) -> p m b a", b=2, a=4)[:, :, :, a], words, a)
                do(ins)
                do(dve.tensor_scalar(dst[0:n, 0:width], raw, 1.0, None, ALU.add))

            def take_zeros(m, width, number):
                dve.wait_ge(gu_in[m], number * 48 + 48)
                unpack_zeros(z_in[m], z_one[m], P, width)

            def unpack_gu(m, c, e, full_count, last_use):
                if full_count is not None:
                    dve.wait_ge(full_ready, full_count)
                if c < NT:
                    i, M = c % 4 + 4 * e, P
                    words = q_in[m][:].bitcast(U16).rearrange("p (r i b) -> p r i b", i=8, b=2)[:, :, i, :]
                    zeros = bass.AP(z_one[m][:].tensor, i, [[1024, P], [0, 4], [8, P], [0, 2]])
                    scales = s_in[m][:].rearrange("p (r i) -> p r i", i=8)[:, :, i]
                else:
                    n0 = 256 * (c - NT) + P * e
                    M = P if 2 * c + e < 2 * NC - 1 else LAST
                    words = q_in[m][:, n0:n0 + M].bitcast(U16).rearrange("p (r b) -> p r b", b=2)
                    zeros = bass.AP(z_one[m][:].tensor, n0, [[1024, P], [0, 4], [1, M], [0, 2]])
                    scales = s_in[m][:, n0:n0 + M]
                whole = diff[m][:].rearrange("p (a r b) -> p a r b", a=4, b=2)[:, :, 0:M, :]
                for a in range(4):
                    nibbles(whole[:, a].bitcast(U16), words, a)
                ins = dve.tensor_copy(s_tile[m][:, 0:M], scales)
                if last_use is not None:
                    ins.then_inc(gu_used[m], 1)
                    dve.wait_ge(gu_used[m], last_use)
                else:
                    do(ins)
                dve.tensor_tensor(whole, whole.bitcast(U16), zeros, ALU.subtract).then_inc(diff_ready, 1)

            def unpack_down(c, e, chunk):
                m, n = f"d{e}", (P if 2 * c + e < 2 * NC - 1 else LAST)
                dve.wait_ge(d_in[e], chunk * 48 + 48)
                dve.wait_ge(full_ready, chunk * 6 + (4 + e))
                dve.wait_ge(diff_ready, chunk * 6 + (3 + e))
                unpack_zeros(zd_in[e], z_one["d"], n, HID)
                q = qd_in[e][0:n, :]
                do(dve.tensor_scalar(q, q, shifts[0:n, 2 * c + e:2 * c + e + 1], 15,
                                     ALU.logical_shift_right, ALU.bitwise_and))
                dve.tensor_tensor(diff[m][0:n, :], q, z_one["d"][0:n, :], ALU.subtract).then_inc(diff_ready, 1)

            def take_mid(c, e, chunk):
                M = P if 2 * c + e < 2 * NC - 1 else LAST
                k = chunk * 4 + 2 * e
                dve.wait_ge(u_mm, chunk * 2 + (e + 2))
                dve.wait_ge(silu_done, chunk * 2 + (e + 2))
                for tb in range(2):
                    dve.tensor_tensor(mid[0:M, tb, :], u_ps[tb][0:M, :], silu[0:M, tb, :], ALU.mult
                                      ).then_inc(mid_done, 1)
                for tb in range(2):
                    dve.wait_ge(mid_cast, k + (tb + 1))
                    dve.wait_ge(mid_done, k + (tb + 2))
                    dve.tensor_tensor(mid_l[0:M, e, 512 * tb:512 * tb + 512], mid[0:M, tb, :],
                                      mid_h[0:M, e, 512 * tb:512 * tb + 512].bitcast(F32), ALU.subtract
                                      ).then_inc(mid_ready, 1)
                dve.wait_ge(mid_ready, k + 2)

            def add_down(c, chunk, i):
                tt, mb = i // 2, i % 2
                dst = acc[:, tt, 512 * mb:512 * mb + 512]
                dve.wait_ge(d_mm, chunk * 16 + (i + 1))
                if c == 0:
                    dve.tensor_copy(dst, d_ps[i % 4][:]).then_inc(acc_done, 1)
                else:
                    dve.wait_ge(acc_done, chunk * 16 + (i + 5 - 16))
                    dve.tensor_tensor(dst, d_ps[i % 4][:], dst, ALU.add).then_inc(acc_done, 1)

            take_zeros("g", 1024, 0)
            unpack_gu("g", 0, 0, None, None)
            take_zeros("u", 1024, 0)
            unpack_gu("u", 0, 0, None, None)
            dve.wait_ge(shifts_in, 16)
            with dve.Fori(0, 2) as hf:
                step.enter(hf, FFN_STEPS)
                for c in range(NC):
                    chunk = hf * NC + c
                    load = {3: 0, 7: 1, NC - 1: 2}.get(c)
                    used = None if load is None else hf * NLOAD + (load + 2)
                    width = {3: 1024, 7: INTER - 2048, NC - 1: 1024}.get(c)
                    unpack_gu("g", c, 1, chunk * 6 + 7, used)
                    if c == 1:
                        dve.wait_ge(out_stored, hf * (16 * HALF // P) + 16)
                    for i in range(16):
                        if c:
                            add_down(c - 1, chunk - 1, i)
                        if i in (3, 8):
                            unpack_down(c, i // 8, chunk)
                        if i == 12:
                            unpack_gu("u", c, 1, chunk * 6 + 8, used)
                    take_mid(c, 0, chunk)
                    if load is not None:
                        take_zeros("g", width, hf * NLOAD + (load + 1))
                    unpack_gu("g", (c + 1) % NC, 0, chunk * 6 + 9, None)
                    if load is not None:
                        take_zeros("u", width, hf * NLOAD + (load + 1))
                    unpack_gu("u", (c + 1) % NC, 0, chunk * 6 + 12, None)
                    take_mid(c, 1, chunk)
                for i in range(16):
                    add_down(NC - 1, hf * NC + (NC - 1), i)
                dve.wait_ge(acc_done, (hf + 1) * (16 * NC) + 4)
                for tt in range(HALF // P):
                    dve.wait_ge(x_fin_in[tt % 2], hf * (8 * HALF // P) + 16 * (tt // 2 + 1))
                    do(dve.tensor_copy(ffn16[:], acc[:, tt, :]))
                    dve.tensor_tensor(acc[:, tt, :], x_fin[:, tt % 2, :], ffn16[:], ALU.add).then_inc(out_ready, 1)
                    dve.wait_ge(out_ready, hf * (HALF // P) + (tt + 1))
                step.leave(2)

        @block.gpsimd
        def _(pool):
            pool.sem_inc(full_ready, 6)
            pool.sem_inc(slot_ready, 2)

            def multiply(m, parity, number, n=P, M=P):
                pool.wait_ge(diff_ready, number)
                pool.wait_ge(slot_ready, number)
                if m in ("g", "u"):
                    dst = w_full[:, parity, :].rearrange("p (a b r) -> p a b r", a=4, b=2)
                    src = diff[m][:].rearrange("p (a r b) -> p a b r", a=4, b=2)
                    sc = bass.AP(s_tile[m][:].tensor, 0, [[P, P], [0, 4], [0, 2], [1, M]])
                    pool.tensor_tensor(dst[:, :, :, 0:M], src[:, :, :, 0:M], sc, ALU.mult).then_inc(full_ready, 1)
                else:
                    pool.tensor_tensor(w_full[0:n, parity, :], diff[m][0:n, :], sd_in[int(m[1])][0:n, :],
                                       ALU.mult).then_inc(full_ready, 1)

            def low(m, parity, number, n=P, M=P):
                pool.wait_ge(high_ready, number)
                if M == P:
                    pool.tensor_tensor(w_l[m][0:n, :], w_full[0:n, parity, :], w_h[m][0:n, :].bitcast(F32),
                                       ALU.subtract).then_inc(slot_ready, 1)
                else:
                    def cut(t):
                        return t.rearrange("p (k r) -> p k r", r=P)[:, :, 0:M]
                    pool.tensor_tensor(cut(w_l[m][:]), cut(w_full[:, parity, :]), cut(w_h[m][:].bitcast(F32)),
                                       ALU.subtract).then_inc(slot_ready, 1)

            def tile_shape(c, k):
                last = c == NC - 1
                return dict(n=LAST if last and k == 2 else P, M=LAST if last and k in (0, 3) else P)

            def tiles(c, chunk):
                def low_before(k):
                    low(ORDER[k - 1], (k - 1) % 2, chunk * 6 + (k + 2), **tile_shape(c, k - 1))

                for k, m in enumerate(ORDER):
                    if k == 4:
                        low_before(k)
                    multiply(m, k % 2, chunk * 6 + (k + 3), **tile_shape(c, k))
                    if k not in (0, 4):
                        low_before(k)
                low(ORDER[5], 1, chunk * 6 + 8)

            multiply("g", 0, 1)
            multiply("u", 1, 2)
            low("g", 0, 1)
            low("u", 1, 2)
            with pool.Fori(0, 2) as hf:
                for k in range(KT):
                    kt = k // 2 + 4 * (k % 2)
                    pool.wait_ge(y_cast, hf * KT + (k + 1))
                    pool.tensor_tensor(y_l[:, kt, :], y_l[:, kt, :].bitcast(F32), y_h[:, kt, :].bitcast(F32),
                                       ALU.subtract).then_inc(y_ready2, 1)
                with pool.Fori(0, NC - 1) as c:
                    tiles(0, hf * NC + c)
                tiles(NC - 1, hf * NC + (NC - 1))

        @block.scalar
        def _(act):
            act.sem_inc(silu_done, 1)
            act.sem_inc(out_stored, 16)

            def high(m, parity, number, n=P, M=P):
                act.wait_ge(full_ready, number + 6)
                if M == P:
                    act.copy(w_h[m][0:n, :], w_full[0:n, parity, :]).then_inc(high_ready, 1)
                else:
                    act.copy(w_h[m][:].rearrange("p (k r) -> p k r", r=P)[:, :, 0:M],
                             w_full[:, parity, :].rearrange("p (k r) -> p k r", r=P)[:, :, 0:M]
                             ).then_inc(high_ready, 1)

            def take_gate(chunk, e, M):
                act.wait_ge(g_mm, chunk * 2 + (e + 1))
                act.wait_ge(mid_done, chunk * 4 + (2 * e + 1))
                for tb in range(2):
                    ins = act.activation(silu[0:M, tb, :], g_ps[tb][0:M, :], ACT.Silu)
                ins.then_inc(silu_done, 1)

            def cast_mid(chunk, e, M):
                for tb in range(2):
                    act.wait_ge(mid_done, chunk * 4 + (2 * e + tb + 2))
                    act.copy(mid_h[0:M, e, 512 * tb:512 * tb + 512], mid[0:M, tb, :]).then_inc(mid_cast, 1)

            def body(c, chunk):
                last = c == NC - 1
                M1 = LAST if last else P
                take_gate(chunk, 0, P)
                act.wait_ge(g_mm, chunk * 2 + 1)
                high("g", 0, chunk * 6 + 3, M=M1)
                act.wait_ge(acc_done, chunk * 16 + 4)
                high("d0", 1, chunk * 6 + 4)
                high("d1", 0, chunk * 6 + 5, n=M1)
                act.wait_ge(u_mm, chunk * 2 + 2)
                high("u", 1, chunk * 6 + 6, M=M1)
                cast_mid(chunk, 0, P)
                take_gate(chunk, 1, M1)
                act.wait_ge(g_mm, chunk * 2 + 2)
                high("g", 0, chunk * 6 + 7)
                cast_mid(chunk, 1, M1)
                act.wait_ge(u_mm, chunk * 2 + 3)
                high("u", 1, chunk * 6 + 8)

            high("g", 0, 1)
            high("u", 1, 2)
            with act.Fori(0, 2) as hf:
                act.wait_ge(u_mm, hf * (2 * NC) + 1)
                order = [k // 2 + 4 * (k % 2) for k in range(KT)]
                for k, kt in enumerate(order):
                    src = bass.AP(ysc.tensor, hf * HALF + kt * TOK, [[PACK * TOK, P], [1, HALF]])
                    act.dma_start(y_l[:, kt, :].bitcast(F32), src).then_inc(y_loaded[k], 16)
                for k, kt in enumerate(order):
                    act.wait_ge(y_loaded[k], hf * 16 + 16)
                    act.copy(y_h[:, kt, :], y_l[:, kt, :].bitcast(F32)).then_inc(y_cast, 1)
                with act.Fori(0, NC - 1) as c:
                    body(0, hf * NC + c)
                body(NC - 1, hf * NC + (NC - 1))

        @block.tensor
        def _(pe):
            pe.sem_inc(u_mm, 1)

            def project(m, ps, M, count, hf=None):
                for k in range(KT):
                    kt = k // 2 + 4 * (k % 2)
                    if hf is not None:
                        pe.wait_ge(y_ready2, hf * KT + (k + 1))
                    for w, ys in ((w_h[m], (y_h, y_l)), (w_l[m], (y_h,))):
                        for y in ys:
                            for tb in range(2):
                                mm = pe.matmul(ps[tb][0:M, :], w[:, P * k:P * k + M],
                                               y[:, kt, 512 * tb:512 * tb + 512],
                                               start=(k == 0 and w is w_h[m] and y is y_h),
                                               stop=(k == KT - 1 and w is w_l[m]))
                mm.then_inc(count, 1)

            def gate(chunk, e, M, number, hf=None):
                pe.wait_ge(slot_ready, number + 2)
                pe.wait_ge(silu_done, chunk * 2 + (e + 1))
                project("g", g_ps, M, g_mm, hf)

            def up(chunk, e, M, number):
                pe.wait_ge(slot_ready, number + 2)
                pe.wait_ge(mid_done, chunk * 4 + (2 * e + 1))
                project("u", u_ps, M, u_mm)

            def down(chunk, K1):
                pe.wait_ge(slot_ready, chunk * 6 + 7)
                pe.wait_ge(mid_ready, chunk * 4 + 4)
                for i in range(16):
                    tt, mb = i // 2, i % 2
                    pe.wait_ge(acc_done, chunk * 16 + (i + 1))
                    for e in range(2):
                        n = P if e == 0 else K1
                        passes = ((mid_h, w_h), (mid_h, w_l), (mid_l, w_h))
                        for j, (mm_, w) in enumerate(passes):
                            mm = pe.matmul(d_ps[i % 4][:], mm_[0:n, e, P * tt:P * tt + P],
                                           w[f"d{e}"][0:n, 512 * mb:512 * mb + 512],
                                           start=(e == 0 and j == 0), stop=(e == 1 and j == 2))
                    mm.then_inc(d_mm, 1)

            def rest(chunk, M1):
                up(chunk, 0, P, chunk * 6 + 2)
                gate(chunk, 1, M1, chunk * 6 + 3)
                up(chunk, 1, M1, chunk * 6 + 6)

            with pe.Fori(0, 2) as hf:
                gate(hf * NC, 0, P, hf * (6 * NC) + 1, hf)
                rest(hf * NC, P)
                with pe.Fori(1, NC - 1) as c:
                    chunk = hf * NC + c
                    gate(chunk, 0, P, chunk * 6 + 1)
                    down(chunk - 1, P)
                    rest(chunk, P)
                chunk = hf * NC + (NC - 1)
                gate(chunk, 0, P, chunk * 6 + 1)
                down(chunk - 1, P)
                rest(chunk, LAST)
                down(chunk, LAST)


_INS = ["x", "itok_B_8_3872", "L0_cond_log_dt", "L0_cond_C", "L0_cond_log_A_real", "L0_cond_A_imag", "L0_cond_D",
        "L0_ffn_gate_qweight", "L0_ffn_gate_scales", "L0_ffn_gate_zeros",
        "L0_ffn_up_qweight", "L0_ffn_up_scales", "L0_ffn_up_zeros",
        "L0_ffn_down_qweight", "L0_ffn_down_scales", "L0_ffn_down_zeros"]


def kernel(**inputs):
    import concourse.bacc as _bacc
    from concourse.bass_utils import run_bass_kernel_spmd as _run

    nc = _bacc.Bacc("TRN2", target_bir_lowering=False, num_devices=1)
    arrays, args = {}, []

    def give(name, a):
        arrays[name] = a
        args.append(nc.dram_tensor(name, a.shape, mybir.dt.from_np(a.dtype), kind="ExternalInput").ap())

    for name in _INS:
        give(f"in_{name}_dram", np.ascontiguousarray(inputs[name]))
    give("const_table", const_table())
    give("shift_table", shift_table())
    give("identity", np.eye(P, dtype=np.float32))
    args.append(nc.dram_tensor("out_0_dram", (B, H, L), F32, kind="ExternalOutput").ap())
    build_program(nc, *args)
    r = _run(nc, [arrays], core_ids=[0])
    return r.results[0]["out_0_dram"]
```

```python
from contextlib import ExitStack

import numpy as np

import concourse.bass as bass
from concourse import mybir

F32 = mybir.dt.float32
F32R = mybir.dt.float32r
F16 = mybir.dt.float16
BF16 = mybir.dt.bfloat16
I32 = mybir.dt.int32
U16 = mybir.dt.uint16
ALU = mybir.AluOpType
ACT = mybir.ActivationFunctionType

P = 128
B, H, L = 32, 64, 1024
NS = 64
HID, INTER, PACK, GROUP = 1024, 2752, 8, 128
KT = L // P
HG = 4
NG = H // HG
HC = 16
NHC = H // HC
CONV_STEPS = 21
FFN_STEPS = 116
TOK = B * H
HALF = TOK // 2
NC = 11
NT = 8
LAST = INTER - NT * 256 - 2 * 256 - P
KPAD = P + L
TRING = 8

MAGIC = float(1.5 * 2 ** 23)
TWO_PI = 2 * np.pi
PI1 = 6.28125
PI2 = float(np.float32(int((TWO_PI - PI1) * 2 ** 21) / 2 ** 21))
PI3 = float(np.float32(TWO_PI - PI1 - PI2))
LN2 = float(np.log(2))
LN2_1 = 0.693359375
LN2_2 = float(np.float32(LN2 - LN2_1))
PI_BELOW = float(np.nextafter(np.float32(np.pi), np.float32(0)))

C_B, C_A, C_LCOL = 0, 32, 64
C_OFFR, C_OFFR_T, C_OFFL, C_OFFL_T, C_NHPI, C_OFFC, C_OFFC_T = 72, 73, 74, 75, 76, 77, 78
C_N = 80


def const_table():
    t = np.zeros((P, C_N), np.float32)
    t[:, C_B:C_B + 32] = np.arange(32)
    t[:, C_A:C_A + 32] = 32 * np.arange(32)
    t[:, C_LCOL:C_LCOL + KT] = P * np.arange(KT)[None, :] + np.arange(P)[:, None]
    real = np.arange(P) < NS
    t[:, C_OFFR] = np.where(real, np.pi / 2, 0)
    t[:, C_OFFR_T] = np.where(real, 0.25, 0)
    t[:, C_OFFL] = np.where(real, np.pi / 2, np.pi)
    t[:, C_OFFL_T] = np.where(real, 0.25, 0.5)
    t[:, C_NHPI] = -np.pi / 2
    t[:, C_OFFC] = np.pi / 2
    t[:, C_OFFC_T] = 0.25
    return t


def shift_table():
    t = np.zeros((P, 2 * NC), np.int32)
    for c in range(NC):
        for e in range(2):
            t[:, 2 * c + e] = 4 * (c % 4 + 4 * e) if c < NT else 4 * (np.arange(P) % 8)
    return t


class Count:

    def __init__(self, sem, start=0):
        self.sem, self.base, self.n, self.sealed = sem, 0, start, None

    def inc(self, ins, by=1):
        ins.then_inc(self.sem, by)
        self.n += by

    def value(self):
        return self.base + self.n if not isinstance(self.base, int) or self.base else self.n

    def enter(self, i, per):
        self.saved = (self.base, self.n, per)
        self.base = self.base + i * per

    def leave(self, times):
        base, n, per = self.saved
        assert self.n - n == per, (self.n - n, per)
        self.base, self.n = base, n + times * per


def build_program(nc, x, itok, log_dt, C, log_A, A_imag, D, gq, gs, gz, uq, us, uz, dq, ds, dz,
                  ctab, stab, ident_in, out):
    kpad = nc.dram_tensor("kernel_padded", (H, KPAD), F32, kind="Internal").ap()
    ysc = nc.dram_tensor("y_scratch", (L, TOK), F32, kind="Internal").ap()
    with ExitStack() as ctx:
        def sb(name, shape, dt=F32):
            return ctx.enter_context(nc.sbuf_tensor(name, shape, dt))

        def sem(name):
            return ctx.enter_context(nc.semaphore(name))

        bank = [ctx.enter_context(nc.psum_tensor(f"bank{i}", [P, 512], F32)) for i in range(8)]

        y_parts = sb("y_parts", [P, 2, KT, HALF], F32R)
        y_l, y_h = y_parts[:, 0], y_parts[:, 1]
        w_h = {m: sb(f"w{m}_h", [P, KT * P], F32R) for m in ("g", "u")}
        w_l = {m: sb(f"w{m}_l", [P, KT * P], F32R) for m in ("g", "u")}
        w_full = sb("w_full", [P, 2, KT * P])
        q_in = {m: sb(f"q{m}_in", [P, 1024], I32) for m in ("g", "u")}
        s_in = {m: sb(f"s{m}_in", [P, 1024], F16) for m in ("g", "u")}
        z_in = {m: sb(f"z{m}_in", [P, 128], I32) for m in ("g", "u")}
        z_one = {m: sb(f"z{m}_one", [P, 1024], BF16) for m in ("g", "u")}
        diff = {m: sb(f"diff_{m}", [P, KT * P], BF16) for m in ("g", "u")}
        s_tile = {m: sb(f"s_tile_{m}", [P, P], F16) for m in ("g", "u")}
        shifts = sb("shifts", [P, 2 * NC], I32)

        with ExitStack() as over:
            def sbo(name, shape, dt=F32):
                return over.enter_context(nc.sbuf_tensor(name, shape, dt))

            tab = sbo("tab", [P, C_N])
            ident = sbo("ident", [P, P])
            iota_l = sbo("iota_l", [P, L])
            mask_row = iota_l
            len_i = sbo("len_i", [P, 1], I32)
            len_col = sbo("len_col", [P, 1])
            lens_i = sbo("lens_i", [P, B], I32)
            lens = sbo("lens", [P, B])
            mask_t = sbo("mask_t", [P, KT, B])
            logs = sbo("logs", [H, 1 + NS])
            exps = sbo("exps", [H, 1 + NS])
            power = sbo("power", [H, 1 + NS])
            power_i = sbo("power_i", [H, 1 + NS], I32)
            rest = sbo("rest", [H, 1 + NS])
            c_in = sbo("c_in", [H, NS, 2])
            ai_in = sbo("ai_in", [H, NS])
            d_row = sbo("d_row", [1, H])
            dt, eA = exps[:, 0:1], exps[:, 1:1 + NS]
            (are, are_arg, aim, exp_are, half_aim, arg_s, arg_c, sn, cs, em1, t1, t2, t3, zr, zi, inv) = (
                sbo(n, [H, NS]) for n in ("are", "are_arg", "aim", "exp_are", "half_aim", "arg_s", "arg_c", "sn",
                                          "cs", "em1", "t1", "t2", "t3", "zr", "zi", "inv"))
            par_h = sbo("par_h", [H, 4, 2, NS])
            par = sbo("par", [P, 4, H])
            (e_r, e_l, th_r, th_l, turns, s_r, p_1, p_2) = (
                sbo(n, [P, HC, 32]) for n in ("e_r", "e_l", "th_r", "th_l", "turns", "s_r", "p_1", "p_2"))
            right, left = th_r, th_l
            k_sb = sbo("k_sb", [32, HC, 32])
            zero = sbo("zero", [H, P])
            toep = sbo("toep", [P, TRING, L])
            x_in, x_rev = toep[:, 0:4, :], toep[:, 4:8, :]
            u_all = y_parts[:].bitcast(F32)
            u_t = sbo("u_t", [P, 2, KT, P])
            y_nat = sbo("y_nat", [P, 2, KT, P])

        for m in ("d0", "d1"):
            w_h[m] = sb(f"w{m}_h", [P, HID], F32R)
            w_l[m] = sb(f"w{m}_l", [P, HID], F32R)
            diff[m] = sb(f"diff_{m}", [P, HID], BF16)
        mid_h = sb("mid_h", [P, 2, HALF], F32R)
        mid_l = sb("mid_l", [P, 2, HALF], F32R)
        acc = sb("acc", [P, HALF // P, HID])
        silu = sb("silu", [P, 2, 512])
        mid = sb("mid", [P, 2, 512])
        qd_in = [sb(f"qd_in{e}", [P, HID], I32) for e in range(2)]
        sd_in = [sb(f"sd_in{e}", [P, HID], F16) for e in range(2)]
        zd_in = [sb(f"zd_in{e}", [P, HID // PACK], I32) for e in range(2)]
        z_one["d"] = sb("zd_one", [P, HID], BF16)
        x_fin = [silu, mid]
        ffn16 = sb("ffn16", [P, 2, HID], F16)

        par_in, tab_in, len_in, lens_in = sem("par_in"), sem("tab_in"), sem("len_in"), sem("lens_in")
        x_loaded = [sem(f"x_loaded{i}") for i in range(4)]
        logs_in, mask_ready, u_all_ready = sem("logs_in"), sem("mask_ready"), sem("u_all_ready")
        t_loaded = [sem(f"t_loaded{i}") for i in range(TRING)]
        y_stored = [sem("y_stored0"), sem("y_stored1")]
        k_stored, zero_stored, const_ready = sem("k_stored"), sem("zero_stored"), sem("const_ready")
        dve_step = sem("dve_step")
        f_args, f_done = sem("f_args"), sem("f_done")
        par_ready, par_turned = sem("par_ready"), sem("par_turned")
        lr_ready, k_mm, k_sb_ready = sem("lr_ready"), sem("k_mm"), sem("k_sb_ready")
        rev_ready, u_turned, u_ready = sem("rev_ready"), sem("u_turned"), sem("u_ready")
        conv_mm, y_ready = sem("conv_mm"), sem("y_ready")

        turn_ps = [bank[0:2], bank[2:4]]
        conv_ps = [bank[2:4], bank[4:6]]
        k_ps, par_ps = bank[6], bank[7]

        shifts_in = sem("shifts_in")
        y0_loaded = [sem(f"y0_loaded{k}") for k in range(KT)]
        y1_loaded = [sem(f"y1_loaded{k}") for k in range(KT)]
        y_cast, y_split = sem("y_cast"), sem("y_split")
        gu_in = {m: sem(f"{m}_in") for m in ("g", "u")}
        gu_used = {m: sem(f"{m}_used") for m in ("g", "u")}
        d_in = [sem(f"d_in{e}") for e in range(2)]
        x_fin_in = [sem("x_fin_in0"), sem("x_fin_in1")]
        ffn16_ready, out_ready, out_stored = sem("ffn16_ready"), sem("out_ready"), sem("out_stored")
        diff_ready, full_ready, high_ready, slot_ready = (
            sem("diff_ready"), sem("full_ready"), sem("high_ready"), sem("slot_ready"))
        g_mm, u_mm, d_mm = sem("g_mm"), sem("u_mm"), sem("d_mm")
        silu_done, mid_done, mid_cast, mid_ready, acc_done = (
            sem("silu_done"), sem("mid_done"), sem("mid_cast"), sem("mid_ready"), sem("acc_done"))

        g_ps, u_ps, d_ps = bank[0:2], bank[2:4], bank[4:8]

        ORDER = ["g", "d0", "d1", "u", "g", "u"]
        NLOAD = 3
        TT = HALF // P

        def x_rows(g):
            return bass.AP(x.tensor, g * (HG * L), [[L, HG], [H * L, B], [1, L]])

        block = ctx.enter_context(nc.Block())

        @block.sync
        def _(sp):
            src = {"g": (gq, gs, gz), "u": (uq, us, uz)}

            def load_gu(m, n0, width, number):
                q, s, z = src[m]
                sp.wait_ge(gu_used[m], number + 1)
                sp.dma_start(q_in[m][:, 0:width], q[:, n0:n0 + width]).then_inc(gu_in[m], 16)
                sp.dma_start(s_in[m][:, 0:width],
                             bass.AP(s.tensor, n0, [[INTER, 8], [0, 16], [1, width]])).then_inc(gu_in[m], 16)
                sp.dma_start(z_in[m][:, 0:width // PACK],
                             bass.AP(z.tensor, n0 // PACK, [[INTER // PACK, 8], [0, 16], [1, width // PACK]])
                             ).then_inc(gu_in[m], 16)

            for y in y_stored:
                sp.sem_inc(y, 16)
            sp.dma_start(logs[:, 0:1], log_dt.rearrange("(h o) -> h o", o=1)).then_inc(logs_in, 16)
            sp.dma_start(logs[:, 1:1 + NS], log_A).then_inc(logs_in, 16)
            sp.dma_start(len_i[:], bass.AP(itok.tensor, 0, [[0, HG], [1, B], [1, 1]])).then_inc(len_in, 16)
            sp.dma_start(ai_in[:], A_imag).then_inc(par_in, 16)
            sp.dma_start(x_in[:, 0, :], x_rows(0)).then_inc(x_loaded[0], 16)
            sp.dma_start(ident[:], ident_in).then_inc(tab_in, 16)
            sp.dma_start(c_in[:], C).then_inc(par_in, 16)
            sp.dma_start(d_row[:], D.rearrange("(o h) -> o h", o=1)).then_inc(par_in, 16)
            sp.dma_start(tab[:], ctab).then_inc(tab_in, 16)
            sp.dma_start(lens_i[:], bass.AP(itok.tensor, 0, [[0, P], [1, B]])).then_inc(lens_in, 16)
            for g in range(1, 4):
                sp.dma_start(x_in[:, g, :], x_rows(g)).then_inc(x_loaded[g], 16)
            with sp.Fori(1, NG // 4) as i:
                for j in range(4):
                    sp.wait_ge(rev_ready, i * 4 + (j - 3))
                    sp.dma_start(x_in[:, j, :], x_rows(i * 4 + j)).then_inc(x_loaded[j], 16)
            sp.dma_start(shifts[:], stab).then_inc(shifts_in, 16)
            load_gu("g", 0, 1024, 0)
            load_gu("u", 0, 1024, 0)
            sp.wait_ge(zero_stored, 16)

            def load_toeplitz(g, half_):
                for hh in range(HG):
                    slot = HG * half_ + hh
                    sp.wait_ge(conv_mm, g * HG + (hh + 1))
                    src = bass.AP(kpad.tensor, (g * HG + hh) * KPAD + 1, [[1, P], [1, L]])
                    sp.dma_start(toep[:, slot, :], src).then_inc(t_loaded[slot], 16)

            def piece(hc, last):
                for q in range(4):
                    g = hc * 4 + q
                    if q == 2 and not last:
                        sp.wait_ge(k_stored, hc * 16 + 32)
                    if not (last and q >= 2):
                        load_toeplitz(g + 2, q % 2)
                    sp.wait_ge(y_ready, g * 2 + 6)
                    dst = bass.AP(ysc.tensor, g * P, [[TOK, P], [P * TOK, KT], [1, P]])
                    sp.dma_start(dst, y_nat[:, q % 2, :, :]).then_inc(y_stored[q % 2], 16)

            sp.wait_ge(u_turned, NG + 4)
            sp.wait_ge(k_stored, 16)
            load_toeplitz(0, 0)
            load_toeplitz(1, 1)
            with sp.Fori(0, NHC - 1) as hc:
                piece(hc, False)
            piece(NHC - 1, True)
            for y in y_stored:
                sp.wait_ge(y, 16 + 16 * NG // 2)

            def load_down(c, e, number):
                sp.wait_ge(full_ready, number * 6 + (4 + e))
                if c < NT:
                    t, n, G = c // 4, P, HID // PACK
                    q_src = dq[P * t:P * t + P, :]
                    s_src = bass.AP(ds.tensor, 8 * t * HID, [[HID, 8], [0, 16], [1, HID]])
                    z_src = bass.AP(dz.tensor, 8 * t * G, [[G, 8], [0, 16], [1, G]])
                else:
                    v = 2 * (c - NT) + e
                    n, G = (P if 2 * c + e < 2 * NC - 1 else LAST), HID // PACK
                    q_src = bass.AP(dq.tensor, (256 + 16 * v) * HID, [[HID, n // 8], [0, 8], [1, HID]])
                    s_src = bass.AP(ds.tensor, (16 + v) * HID, [[0, n], [1, HID]])
                    z_src = bass.AP(dz.tensor, (16 + v) * G, [[0, n], [1, G]])
                sp.dma_start(qd_in[e][0:n, :], q_src).then_inc(d_in[e], 16)
                sp.dma_start(sd_in[e][0:n, :], s_src).then_inc(d_in[e], 16)
                sp.dma_start(zd_in[e][0:n, :], z_src).then_inc(d_in[e], 16)

            for e in range(2):
                load_down(0, e, 0)
            with sp.Fori(0, 2) as hf:
                for c in range(NC):
                    for e in range(2):
                        load_down((c + 1) % NC, e, hf * NC + (c + 1))
                    if c in (3, 7, NC - 1):
                        n0, width = {3: (1024, 1024), 7: (2048, INTER - 2048), NC - 1: (0, 1024)}[c]
                        number = {3: 1, 7: 2, NC - 1: 3}[c]
                        for m in ("g", "u"):
                            load_gu(m, n0, width, hf * NLOAD + number)
                sp.wait_ge(mid_ready, (hf + 1) * (4 * NC))
                for tt in range(2):
                    sp.dma_start(x_fin[tt][:], x_rows(hf * TT + tt)).then_inc(x_fin_in[tt], 16)
                for tt in range(TT):
                    sp.wait_ge(out_ready, hf * TT + (TT + tt + 1))
                    if tt + 2 < TT:
                        sp.dma_start(x_fin[tt % 2][:], x_rows(hf * TT + (tt + 2))).then_inc(x_fin_in[tt % 2], 16)
                    dst = bass.AP(out.tensor, (hf * TT + tt) * (HG * L), [[L, HG], [H * L, B], [1, L]])
                    sp.dma_start(dst, acc[:, tt, :]).then_inc(out_stored, 16)
            sp.wait_ge(out_stored, 16 + 16 * 2 * (HALF // P))
            for e in range(2):
                sp.wait_ge(d_in[e], 48 * (2 * NC + 1))
            for m in ("g", "u"):
                sp.wait_ge(gu_in[m], 48 * (2 * NLOAD + 1))

        @block.gpsimd
        def _(pool):
            pool.iota(iota_l[:], [[1, L]], base=0, channel_multiplier=0,
                      allow_small_or_imprecise_dtypes=True).then_inc(const_ready, 1)
            pool.memset(zero[:], 0.0).then_inc(const_ready, 1)
            pool.wait_ge(const_ready, 2)
            pool.dma_start(kpad[:, 0:P], zero[:]).then_inc(zero_stored, 16)
            pool.wait_ge(mask_ready, 1)
            with pool.Fori(0, NG // 4) as i:
                for j in range(4):
                    pool.wait_ge(x_loaded[j], i * 16 + 16)
                    pool.wait_ge(u_turned, i * 4 + (j + 1))
                    pool.tensor_tensor(x_rev[:, j, :].rearrange("p (c l) -> p c l", c=KT)[:, :, ::-1],
                                       x_in[:, j, :].rearrange("p (c l) -> p c l", c=KT),
                                       mask_row[:].rearrange("p (c l) -> p c l", c=KT), ALU.mult
                                       ).then_inc(rev_ready, 1)
            with pool.Fori(0, NHC) as hc:
                pool.wait_ge(k_sb_ready, hc + 2)
                dst = bass.AP(kpad.tensor, hc * (HC * KPAD) + P, [[32, 32], [KPAD, HC], [1, 32]])
                pool.dma_start(dst, k_sb[:]).then_inc(k_stored, 16)
                pool.wait_ge(k_stored, hc * 16 + 16)
            for y in y_stored:
                pool.wait_ge(y, 16 + 16 * NG // 4)
            for k in range(KT):
                kt = k // 2 + 4 * (k % 2)
                pool.wait_ge(conv_mm, TRING + 50 + k)
                src = bass.AP(ysc.tensor, kt * TOK, [[PACK * TOK, P], [1, HALF]])
                pool.dma_start(y_l[:, kt, :].bitcast(F32), src).then_inc(y0_loaded[k], 16)

            pool.sem_inc(full_ready, 6)
            pool.sem_inc(slot_ready, 2)

            def multiply(m, parity, number, n=P):
                pool.wait_ge(diff_ready, number)
                pool.wait_ge(slot_ready, number)
                if m in ("g", "u"):
                    dst = w_full[:, parity, :].rearrange("p (a b r) -> p a b r", a=4, b=2)
                    src = diff[m][:].rearrange("p (a r b) -> p a b r", a=4, b=2)
                    sc = bass.AP(s_tile[m][:].tensor, 0, [[P, P], [0, 4], [0, 2], [1, P]])
                    pool.tensor_tensor(dst, src, sc, ALU.mult).then_inc(full_ready, 1)
                else:
                    pool.tensor_tensor(w_full[0:n, parity, :], diff[m][0:n, :], sd_in[int(m[1])][0:n, :],
                                       ALU.mult).then_inc(full_ready, 1 if n == P else 2)

            def low(m, parity, number, n=P):
                pool.wait_ge(high_ready, number)
                if n < P:
                    pool.wait_ge(slot_ready, number + 1)
                dst = w_l[m][:] if n == P else w_h[m][n:2 * n, :]
                pool.tensor_tensor(dst, w_full[0:n, parity, :], w_h[m][0:n, :].bitcast(F32), ALU.subtract
                                   ).then_inc(slot_ready, 1 if n == P else 2)

            def tiles(last, chunk):
                def rows(k):
                    return LAST if last and k == 2 else P

                def low_before(k):
                    if not (last and k == 4):
                        low(ORDER[k - 1], (k - 1) % 2, chunk * 6 + (k + 2), n=rows(k - 1))

                for k, m in enumerate(ORDER):
                    if k == 4:
                        low_before(k)
                    if not (last and k == 3):
                        multiply(m, k % 2, chunk * 6 + (k + 3), n=rows(k))
                    if k not in (0, 4):
                        low_before(k)

            multiply("g", 0, 1)
            multiply("u", 1, 2)
            low("g", 0, 1)
            with pool.Fori(0, 2) as hf:
                for k in range(KT):
                    kt = k // 2 + 4 * (k % 2)
                    pool.wait_ge(y_cast, hf * KT + (k + 1))
                    pool.tensor_tensor(y_l[:, kt, :], y_l[:, kt, :].bitcast(F32), y_h[:, kt, :].bitcast(F32),
                                       ALU.subtract).then_inc(y_split, 1)
                low("u", 1, hf * (6 * NC) + 2)
                with pool.Fori(0, NC - 1) as c:
                    tiles(False, hf * NC + c)
                    low("u", 1, (hf * NC + c) * 6 + 8)
                tiles(True, hf * NC + (NC - 1))

        @block.scalar
        def _(act):
            act.sem_inc(u_all_ready, 4)
            act.sem_inc(silu_done, 1)
            act.sem_inc(out_stored, 16)
            act.wait_ge(f_args, 1)
            act.activation(exp_are[:], are_arg[:], ACT.Exp).then_inc(f_done, 1)
            act.wait_ge(f_args, 2)
            act.activation(sn[:], arg_s[:], ACT.Sin).then_inc(f_done, 1)
            act.wait_ge(f_args, 3)
            act.activation(cs[:], arg_c[:], ACT.Sin).then_inc(f_done, 1)

            def functions_right(hc):
                act.wait_ge(f_args, hc * 5 + 4)
                act.activation(e_r[:], e_r[:], ACT.Exp).then_inc(f_done, 1)
                act.wait_ge(f_args, hc * 5 + 5)
                act.activation(e_l[:], e_l[:], ACT.Exp).then_inc(f_done, 1)
                act.wait_ge(f_args, hc * 5 + 6)
                act.activation(s_r[:], s_r[:], ACT.Sin).then_inc(f_done, 1)

            def functions_left(hc):
                act.wait_ge(f_args, hc * 5 + 7)
                act.activation(p_1[:], p_1[:], ACT.Sin).then_inc(f_done, 1)
                act.wait_ge(f_args, hc * 5 + 8)
                act.activation(p_2[:], p_2[:], ACT.Sin, bias=tab[:, C_NHPI:C_NHPI + 1]).then_inc(f_done, 1)

            def take_turned(i):
                for j in range(2):
                    act.wait_ge(u_turned, i * 2 + (j + 5))
                    for k in range(2):
                        dst = bass.AP(u_all.tensor, i * (2 * L) + (j * L + 512 * k), [[2 * KT * HALF, P], [1, 512]])
                        act.copy(dst, turn_ps[j][k][:]).then_inc(u_all_ready, 1)

            def bring(g, half_):
                act.wait_ge(conv_mm, g * HG + 4)
                src = bass.AP(u_all.tensor, g * L, [[2 * KT * HALF, P], [1, L]])
                act.copy(u_t[:, half_, :, :].rearrange("p c r -> p (c r)"), src).then_inc(u_ready, 1)

            def high(m, parity, number, n=P):
                act.wait_ge(full_ready, number + 6)
                act.copy(w_h[m][0:n, :], w_full[0:n, parity, :]).then_inc(high_ready, 1 if n == P else 2)

            def take_gate(chunk, e, fused=False):
                if fused:
                    act.wait_ge(u_mm, chunk * 2 + 3)
                else:
                    act.wait_ge(g_mm, chunk * 2 + (e + 1))
                act.wait_ge(mid_done, chunk * 4 + (2 * e + 1))
                M0, M = (LAST, LAST) if fused else (0, P)
                for tb in range(2):
                    ins = act.activation(silu[M0:M0 + M, tb, :], g_ps[tb][0:M, :], ACT.Silu)
                ins.then_inc(silu_done, 1)

            def cast_mid(chunk, e, fused=False):
                for tb in range(2):
                    act.wait_ge(mid_done, chunk * 4 + (2 * e + tb + 2))
                    for M0 in (0, LAST) if fused else (0,):
                        M = LAST if fused else P
                        ins = act.copy(mid_h[M0:M0 + M, e, 512 * tb:512 * tb + 512], mid[0:M, tb, :])
                    ins.then_inc(mid_cast, 1)

            def body(last, chunk, load_y=False):
                take_gate(chunk, 0)
                act.wait_ge(g_mm, chunk * 2 + 1)
                high("g", 0, chunk * 6 + 3)
                act.wait_ge(acc_done, chunk * 16 + 4)
                high("d0", 1, chunk * 6 + 4)
                high("d1", 0, chunk * 6 + 5, n=LAST if last else P)
                if not last:
                    act.wait_ge(u_mm, chunk * 2 + 2)
                    high("u", 1, chunk * 6 + 6)
                cast_mid(chunk, 0)
                take_gate(chunk, 1, fused=last)
                act.wait_ge(u_mm if last else g_mm, chunk * 2 + (3 if last else 2))
                high("g", 0, chunk * 6 + 7)
                cast_mid(chunk, 1, fused=last)
                if load_y:
                    act.wait_ge(u_mm, 2 * NC + 1)
                    for k, kt in enumerate(order):
                        src = bass.AP(ysc.tensor, HALF + kt * TOK, [[PACK * TOK, P], [1, HALF]])
                        act.dma_start(y_l[:, kt, :].bitcast(F32), src).then_inc(y1_loaded[k], 16)
                act.wait_ge(u_mm, chunk * 2 + 3)
                high("u", 1, chunk * 6 + 8)

            order = [k // 2 + 4 * (k % 2) for k in range(KT)]

            def cast_y(k, loaded):
                act.wait_ge(loaded[k], 16)
                act.copy(y_h[:, order[k], :], y_l[:, order[k], :].bitcast(F32)).then_inc(y_cast, 1)

            def piece(hc, last):
                for q in range(4):
                    g = hc * 4 + q
                    if not (last and q == 3):
                        bring(g + 1, (q + 1) % 2)
                    if not last and q == 0:
                        functions_right(hc + 1)
                    if not last and q == 1:
                        functions_left(hc + 1)
                    if last:
                        if q == 1:
                            high("g", 0, 1)
                        if q == 2:
                            high("u", 1, 2)
                            act.wait_ge(u_ready, NG)
                        if q in (2, 3):
                            for k in range(KT // 2):
                                cast_y(KT // 2 * (q - 2) + k, y0_loaded)

            act.wait_ge(tab_in, 32)
            with act.Fori(0, 3) as i:
                take_turned(i)
            functions_right(0)
            with act.Fori(3, 5) as i:
                take_turned(i)
            functions_left(0)
            with act.Fori(5, NG // 2) as i:
                take_turned(i)
            act.wait_ge(u_all_ready, 2 * NG + 4)
            bring(0, 0)
            with act.Fori(0, NHC - 1) as hc:
                piece(hc, False)
            piece(NHC - 1, True)
            for y in y_stored:
                act.wait_ge(y, 16 + 16 * NG // 2)

            def finish(hf, tt):
                act.wait_ge(acc_done, hf * (16 * NC) + (16 * (NC - 1) + 2 * tt + 6))
                act.wait_ge(out_ready, hf * TT + (TT + tt - 1))
                act.copy(ffn16[:, tt % 2, :], acc[:, tt, :]).then_inc(ffn16_ready, 1)

            for hf in range(2):
                with act.Fori(0, NC - 1) as c:
                    body(False, c + hf * NC)
                body(True, hf * NC + (NC - 1), load_y=hf == 0)
                if hf == 0:
                    for k in range(3):
                        cast_y(k, y1_loaded)
                for tt in range(TT):
                    if hf == 0 and tt + 3 < KT:
                        cast_y(tt + 3, y1_loaded)
                    finish(hf, tt)
                act.wait_ge(out_ready, (hf + 2) * TT)

        @block.vector
        def _(dve):
            step = Count(dve_step)

            def do(ins):
                step.inc(ins)
                dve.wait_ge(dve_step, step.value())

            def col(i):
                return tab[:, i:i + 1]

            dve.sem_inc(lr_ready, 1)
            dve.sem_inc(k_sb_ready, 1)
            dve.sem_inc(y_ready, 4)
            for m in ("g", "u"):
                dve.sem_inc(gu_used[m], 1)
            dve.sem_inc(mid_done, 1)
            dve.sem_inc(acc_done, 4)
            dve.sem_inc(out_ready, TT)
            dve.wait_ge(len_in, 16)
            do(dve.tensor_copy(len_col[:], len_i[:]))
            dve.wait_ge(const_ready, 1)
            dve.tensor_scalar(mask_row[:], iota_l[:], len_col[:, 0:1], None, ALU.is_lt).then_inc(mask_ready, 1)
            dve.wait_ge(logs_in, 32)

            def series(p, r):
                do(dve.tensor_scalar(p, r, 1 / 5040.0, None, ALU.mult))
                for c in (1 / 720.0, 1 / 120.0, 1 / 24.0, 1 / 6.0, 0.5, 1.0):
                    do(dve.scalar_tensor_tensor(out=p, in0=p, scalar=c, in1=r, op0=ALU.add, op1=ALU.mult))

            do(dve.tensor_scalar(logs[:], logs[:], -87.0, 88.0, ALU.max, ALU.min))
            do(dve.tensor_scalar(power[:], logs[:], 1 / LN2, None, ALU.mult))
            do(dve.tensor_scalar(power[:], power[:], MAGIC, MAGIC, ALU.add, ALU.subtract))
            do(dve.scalar_tensor_tensor(out=rest[:], in0=power[:], scalar=-LN2_1, in1=logs[:], op0=ALU.mult, op1=ALU.add))
            do(dve.scalar_tensor_tensor(out=rest[:], in0=power[:], scalar=-LN2_2, in1=rest[:], op0=ALU.mult, op1=ALU.add))
            series(exps[:], rest[:])
            do(dve.tensor_scalar(power_i[:], power[:], 127.0, None, ALU.add))
            do(dve.tensor_scalar(power_i[:], power_i[:], 23, None, ALU.logical_shift_left))
            do(dve.scalar_tensor_tensor(out=exps[:], in0=exps[:], scalar=1.0, in1=power_i[:].bitcast(F32),
                                        op0=ALU.add, op1=ALU.mult))
            dve.wait_ge(par_in, 48)
            dve.wait_ge(tab_in, 32)
            do(dve.tensor_scalar(are[:], eA, dt, -1.0, ALU.mult, ALU.mult))
            dve.tensor_copy(are_arg[:], are[:]).then_inc(f_args, 1)
            do(dve.tensor_scalar(aim[:], ai_in[:], dt, None, ALU.mult))
            do(dve.tensor_scalar(half_aim[:], aim[:], 0.5, None, ALU.mult))
            for arg, quarter in ((arg_s, 0.0), (arg_c, 0.25)):
                do(dve.tensor_scalar(t1[:], half_aim[:], 1 / TWO_PI, quarter, ALU.mult, ALU.add))
                do(dve.tensor_scalar(t1[:], t1[:], MAGIC, MAGIC, ALU.add, ALU.subtract))
                do(dve.scalar_tensor_tensor(out=arg[:], in0=t1[:], scalar=-PI1, in1=half_aim[:], op0=ALU.mult, op1=ALU.add))
                do(dve.scalar_tensor_tensor(out=arg[:], in0=t1[:], scalar=-PI2, in1=arg[:], op0=ALU.mult, op1=ALU.add))
                do(dve.scalar_tensor_tensor(out=arg[:], in0=t1[:], scalar=-PI3, in1=arg[:], op0=ALU.mult, op1=ALU.add))
                do(dve.tensor_scalar(arg[:], arg[:], quarter * TWO_PI, PI_BELOW, ALU.add, ALU.min))
                dve.tensor_scalar(arg[:], arg[:], -PI_BELOW, None, ALU.max).then_inc(f_args, 1)
            do(dve.tensor_scalar(t2[:], are[:], -0.25, 0.25, ALU.max, ALU.min))
            series(em1[:], t2[:])
            dve.wait_ge(f_done, 3)
            do(dve.tensor_scalar(t1[:], exp_are[:], 1.0, None, ALU.subtract))
            do(dve.tensor_tensor(t2[:], t2[:], are[:], ALU.is_equal))
            do(dve.tensor_tensor(em1[:], em1[:], t2[:], ALU.mult))
            do(dve.tensor_scalar(t2[:], t2[:], -1.0, 1.0, ALU.mult, ALU.add))
            do(dve.tensor_tensor(t1[:], t1[:], t2[:], ALU.mult))
            do(dve.tensor_tensor(em1[:], em1[:], t1[:], ALU.add))
            do(dve.scalar_tensor_tensor(out=t1[:], in0=sn[:], scalar=-2.0, in1=sn[:], op0=ALU.mult, op1=ALU.mult))
            do(dve.scalar_tensor_tensor(out=t2[:], in0=t1[:], scalar=1.0, in1=em1[:], op0=ALU.add, op1=ALU.mult))
            do(dve.tensor_tensor(t1[:], t1[:], t2[:], ALU.add))
            do(dve.scalar_tensor_tensor(out=t2[:], in0=sn[:], scalar=2.0, in1=cs[:], op0=ALU.mult, op1=ALU.mult))
            do(dve.tensor_tensor(t2[:], t2[:], exp_are[:], ALU.mult))
            do(dve.tensor_tensor(inv[:], eA, eA, ALU.mult))
            do(dve.tensor_tensor(t3[:], ai_in[:], ai_in[:], ALU.mult))
            do(dve.tensor_tensor(inv[:], inv[:], t3[:], ALU.add))
            do(dve.reciprocal(inv[:], inv[:]))
            do(dve.tensor_tensor(zr[:], t2[:], ai_in[:], ALU.mult))
            do(dve.tensor_tensor(t3[:], t1[:], eA, ALU.mult))
            do(dve.tensor_tensor(zr[:], zr[:], t3[:], ALU.subtract))
            do(dve.tensor_tensor(zr[:], zr[:], inv[:], ALU.mult))
            do(dve.tensor_tensor(zi[:], t2[:], eA, ALU.mult))
            do(dve.tensor_tensor(t3[:], t1[:], ai_in[:], ALU.mult))
            do(dve.scalar_tensor_tensor(out=zi[:], in0=zi[:], scalar=-1.0, in1=t3[:], op0=ALU.mult, op1=ALU.subtract))
            do(dve.tensor_tensor(zi[:], zi[:], inv[:], ALU.mult))
            cr, ci = c_in[:, :, 0], c_in[:, :, 1]
            do(dve.tensor_tensor(t1[:], cr, zr[:], ALU.mult))
            do(dve.tensor_tensor(t2[:], ci, zi[:], ALU.mult))
            do(dve.tensor_tensor(t1[:], t1[:], t2[:], ALU.subtract))
            do(dve.tensor_tensor(t2[:], cr, zi[:], ALU.mult))
            do(dve.tensor_tensor(t3[:], ci, zr[:], ALU.mult))
            do(dve.tensor_tensor(t2[:], t2[:], t3[:], ALU.add))
            for n in range(2):
                dve.tensor_copy(par_h[:, 0, n, :], are[:]).then_inc(par_ready, 1)
                dve.tensor_copy(par_h[:, 1, n, :], aim[:]).then_inc(par_ready, 1)
                dve.tensor_scalar(par_h[:, 2, n, :], t1[:], 2.0, None, ALU.mult).then_inc(par_ready, 1)
                dve.tensor_scalar(par_h[:, 3, n, :], t2[:], 2.0, None, ALU.mult).then_inc(par_ready, 1)
            dve.wait_ge(par_turned, 1)
            do(dve.tensor_copy(par[:], par_ps[:, 0:4 * H].rearrange("p (v h) -> p v h", v=4)))

            def wide(v, hc):
                return bass.AP(par[:].tensor, hc * HC + v * H, [[4 * H, P], [1, HC], [0, 32]])

            def exponents(c0):
                return bass.AP(tab[:].tensor, c0, [[C_N, P], [0, HC], [1, 32]])

            def arguments(hc):
                dve.wait_ge(lr_ready, hc + 1)
                dve.wait_ge(k_mm, hc + 1)
                dve.tensor_tensor(e_r[:], wide(0, hc), exponents(C_B), ALU.mult).then_inc(f_args, 1)
                dve.tensor_tensor(e_l[:], wide(0, hc), exponents(C_A), ALU.mult).then_inc(f_args, 1)
                dve.tensor_tensor(th_r[:], wide(1, hc), exponents(C_B), ALU.mult)
                do(dve.tensor_tensor(th_l[:], wide(1, hc), exponents(C_A), ALU.mult))

            def reduce(arg, th, off, off_t):
                do(dve.tensor_scalar(turns[:], th[:], 1 / TWO_PI, None, ALU.mult))
                do(dve.tensor_scalar(turns[:], turns[:], col(off_t), None, ALU.add))
                do(dve.tensor_scalar(turns[:], turns[:], MAGIC, MAGIC, ALU.add, ALU.subtract))
                do(dve.scalar_tensor_tensor(out=arg[:], in0=turns[:], scalar=-PI1, in1=th[:], op0=ALU.mult, op1=ALU.add))
                do(dve.scalar_tensor_tensor(out=arg[:], in0=turns[:], scalar=-PI2, in1=arg[:], op0=ALU.mult, op1=ALU.add))
                do(dve.scalar_tensor_tensor(out=arg[:], in0=turns[:], scalar=-PI3, in1=arg[:], op0=ALU.mult, op1=ALU.add))
                do(dve.tensor_scalar(arg[:], arg[:], col(off), None, ALU.add))

            def reduce_right():
                reduce(s_r, th_r, C_OFFR, C_OFFR_T)
                dve.tensor_scalar(s_r[:], s_r[:], -PI_BELOW, PI_BELOW, ALU.max, ALU.min).then_inc(f_args, 1)

            def reduce_left():
                reduce(p_1, th_l, C_OFFL, C_OFFL_T)
                do(dve.tensor_scalar(p_1[:], p_1[:], -PI_BELOW, PI_BELOW, ALU.max, ALU.min))
                do(dve.scalar_tensor_tensor(out=p_2[:], in0=p_1[:], scalar=-1.0, in1=p_1[:], op0=ALU.mult, op1=ALU.max))
                dve.sem_inc(f_args, 2)

            def combine(hc):
                dve.wait_ge(f_done, hc * 5 + 8)
                dve.tensor_tensor(right[:], e_r[:], s_r[:], ALU.mult)
                do(dve.tensor_tensor(p_1[:], p_1[:], wide(2, hc), ALU.mult))
                do(dve.tensor_tensor(p_2[:], p_2[:], wide(3, hc), ALU.mult))
                do(dve.tensor_tensor(p_1[:], p_1[:], p_2[:], ALU.subtract))
                dve.tensor_tensor(left[:], p_1[:], e_l[:], ALU.mult).then_inc(lr_ready, 1)

            def take_kernel(hc):
                dve.wait_ge(k_mm, hc + 2)
                if not (isinstance(hc, int) and hc == 0):
                    dve.wait_ge(k_stored, hc * 16)
                do(dve.tensor_copy(k_sb[:], k_ps[0:32, :].rearrange("p (h b) -> p h b", h=HC)))
                d_piece = bass.AP(d_row[:].tensor, hc * HC, [[H, 1], [1, HC], [1, 1]])
                dve.tensor_tensor(k_sb[0:1, :, 0:1], k_sb[0:1, :, 0:1], d_piece, ALU.add).then_inc(k_sb_ready, 1)

            def take_conv(g, half_):
                dve.wait_ge(y_stored[half_], (g - half_) * 8 + 16)
                for k in range(2):
                    dve.wait_ge(conv_mm, g * HG + (TRING + 2 * k + 2))
                    dve.tensor_tensor(
                        y_nat[:, half_, :, 64 * k:64 * k + 64].rearrange("p c (h b) -> p h c b", h=2),
                        conv_ps[half_][k][:].rearrange("p (h c b) -> p h c b", h=2, c=KT),
                        bass.AP(mask_t[:].tensor, 0, [[KT * B, P], [0, 2], [B, KT], [1, B]]),
                        ALU.mult).then_inc(y_ready, 1)

            def nibbles(dst, src_, a):
                return dve.tensor_scalar(dst, src_, 4 * a, 15, ALU.logical_shift_right, ALU.bitwise_and)

            def unpack_zeros(z, dst, n, width):
                words = z[0:n, 0:width // PACK].bitcast(U16).rearrange("p (m b) -> p m b", b=2)
                raw = dst[0:n, 0:width].bitcast(U16)
                for a in range(4):
                    ins = nibbles(raw.rearrange("p (m b a) -> p m b a", b=2, a=4)[:, :, :, a], words, a)
                do(ins)
                do(dve.tensor_scalar(dst[0:n, 0:width], raw, 1.0, None, ALU.add))

            def take_zeros(m, width, number):
                dve.wait_ge(gu_in[m], number * 48 + 48)
                unpack_zeros(z_in[m], z_one[m], P, width)

            def unpack_gu(m, c, e, full_count, last_use, into=None):
                m0, into = (0, m) if into is None else (LAST, into)
                if full_count is not None:
                    dve.wait_ge(full_ready, full_count)
                if c < NT:
                    i, M = c % 4 + 4 * e, P
                    words = q_in[m][:].bitcast(U16).rearrange("p (r i b) -> p r i b", i=8, b=2)[:, :, i, :]
                    zeros = bass.AP(z_one[m][:].tensor, i, [[1024, P], [0, 4], [8, P], [0, 2]])
                    scales = s_in[m][:].rearrange("p (r i) -> p r i", i=8)[:, :, i]
                else:
                    n0 = 256 * (c - NT) + P * e
                    M = P if 2 * c + e < 2 * NC - 1 else LAST
                    words = q_in[m][:, n0:n0 + M].bitcast(U16).rearrange("p (r b) -> p r b", b=2)
                    zeros = bass.AP(z_one[m][:].tensor, n0, [[1024, P], [0, 4], [1, M], [0, 2]])
                    scales = s_in[m][:, n0:n0 + M]
                whole = diff[into][:].rearrange("p (a r b) -> p a r b", a=4, b=2)[:, :, m0:m0 + M, :]
                for a in range(4):
                    nibbles(whole[:, a].bitcast(U16), words, a)
                ins = dve.tensor_copy(s_tile[into][:, m0:m0 + M], scales)
                if last_use is not None:
                    ins.then_inc(gu_used[m], 1)
                    dve.wait_ge(gu_used[m], last_use)
                else:
                    do(ins)
                ins = dve.tensor_tensor(whole, whole.bitcast(U16), zeros, ALU.subtract)
                if M == P or m0:
                    ins.then_inc(diff_ready, 1)

            def unpack_down(c, e, chunk):
                m, n = f"d{e}", (P if 2 * c + e < 2 * NC - 1 else LAST)
                dve.wait_ge(d_in[e], chunk * 48 + 48)
                dve.wait_ge(full_ready, chunk * 6 + (4 + e))
                dve.wait_ge(diff_ready, chunk * 6 + (3 + e))
                unpack_zeros(zd_in[e], z_one["d"], n, HID)
                q = qd_in[e][0:n, :]
                do(dve.tensor_scalar(q, q, shifts[0:n, 2 * c + e:2 * c + e + 1], 15,
                                     ALU.logical_shift_right, ALU.bitwise_and))
                dve.tensor_tensor(diff[m][0:n, :], q, z_one["d"][0:n, :], ALU.subtract
                                  ).then_inc(diff_ready, 1 if n == P else 2)

            def take_mid(c, e, chunk):
                M = P if 2 * c + e < 2 * NC - 1 else LAST
                k = chunk * 4 + 2 * e
                dve.wait_ge(u_mm, chunk * 2 + (e + 2))
                dve.wait_ge(silu_done, chunk * 2 + (e + 2))
                for tb in range(2):
                    if M == P:
                        dve.tensor_tensor(mid[:, tb, :], u_ps[tb][:], silu[:, tb, :], ALU.mult).then_inc(mid_done, 1)
                    else:
                        dve.tensor_tensor(mid[0:M, tb, :], g_ps[tb][M:P, :], silu[M:P, tb, :], ALU.mult
                                          ).then_inc(mid_done, 1)
                for tb in range(2):
                    dve.wait_ge(mid_cast, k + (tb + 1))
                    dve.wait_ge(mid_done, k + (tb + 2))
                    dve.tensor_tensor(mid_l[0:M, e, 512 * tb:512 * tb + 512], mid[0:M, tb, :],
                                      mid_h[0:M, e, 512 * tb:512 * tb + 512].bitcast(F32), ALU.subtract
                                      ).then_inc(mid_ready, 1)
                dve.wait_ge(mid_ready, k + 2)

            def add_down(c, chunk, i):
                tt, mb = i // 2, i % 2
                dst = acc[:, tt, 512 * mb:512 * mb + 512]
                dve.wait_ge(d_mm, chunk * 16 + (i + 1))
                if c == 0:
                    dve.tensor_copy(dst, d_ps[i % 4][:]).then_inc(acc_done, 1)
                else:
                    dve.wait_ge(acc_done, chunk * 16 + (i + 5 - 16))
                    dve.tensor_tensor(dst, d_ps[i % 4][:], dst, ALU.add).then_inc(acc_done, 1)

            arguments(0)
            reduce_right()
            reduce_left()
            dve.wait_ge(lens_in, 16)
            do(dve.tensor_copy(lens[:], lens_i[:]))
            for c in range(KT):
                dve.tensor_scalar(mask_t[:, c, :], lens[:], col(C_LCOL + c), None, ALU.is_gt)
            combine(0)
            take_kernel(0)

            def piece(hc, last):
                for q in range(4):
                    g = hc * 4 + q
                    if q == 0 and not last:
                        arguments(hc + 1)
                        reduce_right()
                    if q == 1 and not last:
                        reduce_left()
                    if q == 2 and not last:
                        take_kernel(hc + 1)
                    if q == 1 and not last:
                        combine(hc + 1)
                    take_conv(g, q % 2)
                    if last and q < 2:
                        m = "gu"[q]
                        take_zeros(m, 1024, 0)
                        unpack_gu(m, 0, 0, None, None)

            with dve.Fori(0, NHC - 1) as hc:
                step.enter(hc, CONV_STEPS)
                piece(hc, False)
                step.leave(NHC - 1)
            piece(NHC - 1, True)

            def finish(hf, tt):
                dve.wait_ge(x_fin_in[tt % 2], hf * (8 * TT) + 16 * (tt // 2 + 1))
                dve.wait_ge(ffn16_ready, hf * TT + (tt + 1))
                dve.tensor_tensor(acc[:, tt, :], x_fin[tt % 2][:].rearrange("p a b -> p (a b)"), ffn16[:, tt % 2, :], ALU.add
                                  ).then_inc(out_ready, 1)

            dve.wait_ge(shifts_in, 16)
            with dve.Fori(0, 2) as hf:
                step.enter(hf, FFN_STEPS)
                for c in range(NC):
                    chunk = hf * NC + c
                    load = {3: 0, 7: 1, NC - 1: 2}.get(c)
                    used = None if load is None else hf * NLOAD + (load + 2)
                    width = {3: 1024, 7: INTER - 2048, NC - 1: 1024}.get(c)
                    last = c == NC - 1
                    unpack_gu("g", c, 1, chunk * 6 + 7, used)
                    if last:
                        unpack_gu("u", c, 1, None, used, into="g")
                    if c == 1:
                        dve.wait_ge(out_stored, hf * (16 * HALF // P) + 16)
                    for i in range(16):
                        if c:
                            add_down(c - 1, chunk - 1, i)
                        if i in (3, 8):
                            unpack_down(c, i // 8, chunk)
                        if i == 12 and not last:
                            unpack_gu("u", c, 1, chunk * 6 + 8, used)
                    take_mid(c, 0, chunk)
                    if load is not None:
                        take_zeros("g", width, hf * NLOAD + (load + 1))
                    unpack_gu("g", (c + 1) % NC, 0, chunk * 6 + 9, None)
                    if load is not None:
                        take_zeros("u", width, hf * NLOAD + (load + 1))
                    unpack_gu("u", (c + 1) % NC, 0, chunk * 6 + 12, None)
                    take_mid(c, 1, chunk)
                for i in range(16):
                    add_down(NC - 1, hf * NC + (NC - 1), i)
                    if i % 2 == 1 and i > 1:
                        finish(hf, i // 2 - 1)
                finish(hf, TT - 1)
                dve.wait_ge(out_ready, hf * TT + 2 * TT)
                step.leave(2)

        @block.tensor
        def _(pe):
            pe.sem_inc(k_mm, 1)
            pe.sem_inc(u_mm, 1)
            pe.sem_inc(u_turned, 4)
            pe.sem_inc(conv_mm, TRING)
            pe.wait_ge(tab_in, 32)

            def turn(g, j):
                pe.wait_ge(rev_ready, g + 1)
                pe.wait_ge(u_all_ready, g * 2 + 2)
                for c in range(KT):
                    mm = pe.transpose(turn_ps[j % 2][c // 4][:, P * (c % 4):P * (c % 4) + P],
                                      x_rev[:, j, P * c:P * c + P], ident[:])
                mm.then_inc(u_turned, 1)

            for g in range(4):
                turn(g, g)
            pe.wait_ge(par_ready, 8)
            for v in range(4):
                mm = pe.transpose(par_ps[:, v * H:(v + 1) * H], par_h[:, v, :, :].rearrange("p n s -> p (n s)"),
                                  ident[0:H, 0:H])
            mm.then_inc(par_turned, 1)
            with pe.Fori(1, NG // 4) as i:
                for j in range(4):
                    turn(i * 4 + j, j)

            def multiply_kernel(hc):
                pe.wait_ge(lr_ready, hc + 2)
                pe.wait_ge(k_sb_ready, hc + 1)
                for h in range(HC):
                    mm = pe.matmul(k_ps[0:32, 32 * h:32 * h + 32], left[:, h, :], right[:, h, :],
                                   start=True, stop=True)
                mm.then_inc(k_mm, 1)

            def convolve(hc, q, last):
                g, half_ = hc * 4 + q, q % 2
                pe.wait_ge(u_ready, g + 1)
                for hh in range(HG):
                    if q == 2 and hh == 0 and not last:
                        multiply_kernel(hc + 1)
                    n = HG * q + hh
                    slot, k = n % TRING, hh // 2
                    pe.wait_ge(t_loaded[slot], hc * (16 * HC // TRING) + 16 * (n // TRING + 1))
                    if hh % 2 == 0:
                        pe.wait_ge(y_ready, g * 2 + (k + 1))
                    base = 256 * (hh % 2)
                    for d in range(KT):
                        mm = pe.matmul(
                            conv_ps[half_][k][:, base + B * d:base + 256],
                            toep[:, slot, P * d:P * d + P],
                            u_t[:, half_, 0:KT - d, B * hh:B * hh + B],
                            start=(d == 0), stop=(d == KT - 1))
                    mm.then_inc(conv_mm, 1)

            multiply_kernel(0)

            def piece(hc, last):
                for q in range(4):
                    convolve(hc, q, last)

            with pe.Fori(0, NHC - 1) as hc:
                piece(hc, False)
            piece(NHC - 1, True)


            def project(m, ps, count, hf=None, fused=False):
                for k in range(KT):
                    kt = k // 2 + 4 * (k % 2)
                    if hf is not None:
                        pe.wait_ge(y_split, hf * KT + (k + 1))
                    for w, ys in ((w_h[m], (y_h, y_l)), (w_l[m], (y_h,))):
                        for y in ys:
                            for tb in range(2):
                                before = mm if k else None
                                mm = pe.matmul(ps[tb][:], w[:, P * k:P * k + P], y[:, kt, 512 * tb:512 * tb + 512],
                                               start=(k == 0 and w is w_h[m] and y is y_h),
                                               stop=(k == KT - 1 and w is w_l[m]))
                if fused:
                    before.then_inc(g_mm, 1)
                mm.then_inc(count, 1)

            def gate(chunk, e, number, hf=None, fused=False):
                pe.wait_ge(slot_ready, number + 2)
                pe.wait_ge(silu_done, chunk * 2 + (e + 1))
                project("g", g_ps, u_mm if fused else g_mm, hf, fused)

            def up(chunk, e, number):
                pe.wait_ge(slot_ready, number + 2)
                pe.wait_ge(mid_done, chunk * 4 + (2 * e + 1))
                project("u", u_ps, u_mm)

            def down(chunk, last):
                pe.wait_ge(slot_ready, chunk * 6 + 7)
                if not last:
                    pe.wait_ge(mid_ready, chunk * 4 + 4)
                passes = [[(mid_h, w_h, P), (mid_h, w_l, P), (mid_l, w_h, P)] for e in range(2)]
                if last:
                    passes[1] = [(mid_h, w_h, P), (mid_l, w_h, LAST)]

                def output(i, e):
                    tt, mb = i // 2, i % 2
                    if e == 0:
                        pe.wait_ge(acc_done, chunk * 16 + (i + 1))
                    for j, (m_, w, n) in enumerate(passes[e]):
                        mm = pe.matmul(d_ps[i % 4][:], m_[0:n, e, P * tt:P * tt + P],
                                       w[f"d{e}"][0:n, 512 * mb:512 * mb + 512],
                                       start=(e == 0 and j == 0), stop=(e == 1 and j == len(passes[1]) - 1))
                    if e == 1:
                        mm.then_inc(d_mm, 1)

                ahead = 4 if last else 0
                if last:
                    pe.wait_ge(mid_ready, chunk * 4 + 2)
                    for i in range(ahead):
                        output(i, 0)
                    pe.wait_ge(mid_ready, chunk * 4 + 4)
                for i in range(16):
                    if i >= ahead:
                        output(i, 0)
                    output(i, 1)

            def rest_of(chunk, last):
                up(chunk, 0, chunk * 6 + 2)
                gate(chunk, 1, chunk * 6 + 3, fused=last)
                if not last:
                    up(chunk, 1, chunk * 6 + 6)

            pe.wait_ge(y_ready, 2 * NG + 2)
            with pe.Fori(0, 2) as hf:
                gate(hf * NC, 0, hf * (6 * NC) + 1, hf)
                rest_of(hf * NC, False)
                with pe.Fori(1, NC - 1) as c:
                    chunk = hf * NC + c
                    gate(chunk, 0, chunk * 6 + 1)
                    down(chunk - 1, False)
                    rest_of(chunk, False)
                chunk = hf * NC + (NC - 1)
                gate(chunk, 0, chunk * 6 + 1)
                down(chunk - 1, False)
                rest_of(chunk, True)
                down(chunk, True)


_INS = ["x", "itok_B_8_3872", "L0_cond_log_dt", "L0_cond_C", "L0_cond_log_A_real", "L0_cond_A_imag", "L0_cond_D",
        "L0_ffn_gate_qweight", "L0_ffn_gate_scales", "L0_ffn_gate_zeros",
        "L0_ffn_up_qweight", "L0_ffn_up_scales", "L0_ffn_up_zeros",
        "L0_ffn_down_qweight", "L0_ffn_down_scales", "L0_ffn_down_zeros"]


def kernel(**inputs):
    import concourse.bacc as _bacc
    from concourse.bass_utils import run_bass_kernel_spmd as _run

    nc = _bacc.Bacc("TRN2", target_bir_lowering=False, num_devices=1)
    arrays, args = {}, []

    def give(name, a):
        arrays[name] = a
        args.append(nc.dram_tensor(name, a.shape, mybir.dt.from_np(a.dtype), kind="ExternalInput").ap())

    for name in _INS:
        give(f"in_{name}_dram", np.ascontiguousarray(inputs[name]))
    give("const_table", const_table())
    give("shift_table", shift_table())
    give("identity", np.eye(P, dtype=np.float32))
    args.append(nc.dram_tensor("out_0_dram", (B, H, L), F32, kind="ExternalOutput").ap())
    build_program(nc, *args)
    r = _run(nc, [arrays], core_ids=[0])
    return r.results[0]["out_0_dram"]
```

```python
from contextlib import ExitStack

import numpy as np

import concourse.bass as bass
from concourse import mybir

F32 = mybir.dt.float32
F32R = mybir.dt.float32r
F16 = mybir.dt.float16
BF16 = mybir.dt.bfloat16
I32 = mybir.dt.int32
U16 = mybir.dt.uint16
ALU = mybir.AluOpType
ACT = mybir.ActivationFunctionType

P = 128
B, H, L = 32, 64, 1024
NS = 64
HID, INTER, PACK, GROUP = 1024, 2752, 8, 128
KT = L // P
HG = 4
NG = H // HG
HC = 16
NHC = H // HC
CONV_STEPS = 19
FFN_STEPS = 116
TOK = B * H
HALF = TOK // 2
NC = 11
NT = 8
LAST = INTER - NT * 256 - 2 * 256 - P
KPAD = P + L
POOL_G = 12
TRING = 8

MAGIC = float(1.5 * 2 ** 23)
TWO_PI = 2 * np.pi
PI1 = 6.28125
PI2 = float(np.float32(int((TWO_PI - PI1) * 2 ** 21) / 2 ** 21))
PI3 = float(np.float32(TWO_PI - PI1 - PI2))
LN2 = float(np.log(2))
LN2_1 = 0.693359375
LN2_2 = float(np.float32(LN2 - LN2_1))
PI_BELOW = float(np.nextafter(np.float32(np.pi), np.float32(0)))

C_B, C_A, C_LCOL = 0, 32, 64
C_OFFR, C_OFFR_T, C_OFFL, C_OFFL_T, C_NHPI = 72, 73, 74, 75, 76
C_N = 80


def const_table():
    t = np.zeros((P, C_N), np.float32)
    t[:, C_B:C_B + 32] = np.arange(32)
    t[:, C_A:C_A + 32] = 32 * np.arange(32)
    t[:, C_LCOL:C_LCOL + KT] = P * np.arange(KT)[None, :] + np.arange(P)[:, None]
    real = np.arange(P) < NS
    t[:, C_OFFR] = np.where(real, np.pi / 2, 0)
    t[:, C_OFFR_T] = np.where(real, 0.25, 0)
    t[:, C_OFFL] = np.where(real, np.pi / 2, np.pi)
    t[:, C_OFFL_T] = np.where(real, 0.25, 0.5)
    t[:, C_NHPI] = -np.pi / 2
    return t


def shift_table():
    t = np.zeros((P, 2 * NC), np.int32)
    for c in range(NC):
        for e in range(2):
            t[:, 2 * c + e] = 4 * (c % 4 + 4 * e) if c < NT else 4 * (np.arange(P) % 8)
    return t


class Count:

    def __init__(self, sem):
        self.sem, self.base, self.n = sem, 0, 0

    def inc(self, ins):
        ins.then_inc(self.sem, 1)
        self.n += 1

    def value(self):
        return self.base + self.n

    def enter(self, i, per):
        self.before = (self.base, self.n, per)
        self.base = self.base + i * per

    def leave(self, times):
        base, n, per = self.before
        assert self.n - n == per, (self.n - n, per)
        self.base, self.n = base, n + times * per


def build_program(nc, x, itok, log_dt, C, log_A, A_imag, D, gq, gs, gz, uq, us, uz, dq, ds, dz,
                  ctab, stab, ident_in, out):
    kpad = nc.dram_tensor("kernel_padded", (H, KPAD), F32, kind="Internal").ap()
    ysc = nc.dram_tensor("y_scratch", (L, TOK), F32, kind="Internal").ap()
    with ExitStack() as ctx:
        def sb(name, shape, dt=F32):
            return ctx.enter_context(nc.sbuf_tensor(name, shape, dt))

        def sem(name):
            return ctx.enter_context(nc.semaphore(name))

        bank = [ctx.enter_context(nc.psum_tensor(f"bank{i}", [P, 512], F32)) for i in range(8)]

        y_parts = sb("y_parts", [P, 2, KT, HALF], F32R)
        y_l, y_h = y_parts[:, 0], y_parts[:, 1]
        w_h = {m: sb(f"w{m}_h", [P, KT * P], F32R) for m in ("g", "u")}
        w_l = {m: sb(f"w{m}_l", [P, KT * P], F32R) for m in ("g", "u")}
        w_full = sb("w_full", [P, 2, KT * P])
        q_in = {m: sb(f"q{m}_in", [P, 1024], I32) for m in ("g", "u")}
        s_in = {m: sb(f"s{m}_in", [P, 1024], F16) for m in ("g", "u")}
        z_in = {m: sb(f"z{m}_in", [P, 128], I32) for m in ("g", "u")}
        z_one = {m: sb(f"z{m}_one", [P, 1024], BF16) for m in ("g", "u")}
        diff = {m: sb(f"diff_{m}", [P, KT * P], BF16) for m in ("g", "u")}
        s_tile = {m: sb(f"s_tile_{m}", [P, P], F16) for m in ("g", "u")}
        shifts = sb("shifts", [P, 2 * NC], I32)

        with ExitStack() as over:
            def sbo(name, shape, dt=F32):
                return over.enter_context(nc.sbuf_tensor(name, shape, dt))

            tab = sbo("tab", [P, C_N])
            ident = sbo("ident", [P, P])
            iota_l = sbo("iota_l", [P, L])
            mask_row = iota_l
            len_i = sbo("len_i", [P, 1], I32)
            len_col = sbo("len_col", [P, 1])
            lens_i = sbo("lens_i", [P, B], I32)
            lens = sbo("lens", [P, B])
            mask_t = sbo("mask_t", [P, KT, B])
            logs = sbo("logs", [H, 1 + NS])
            exps = sbo("exps", [H, 1 + NS])
            power = sbo("power", [H, 1 + NS])
            power_i = sbo("power_i", [H, 1 + NS], I32)
            rest = sbo("rest", [H, 1 + NS])
            c_in = sbo("c_in", [H, NS, 2])
            ai_in = sbo("ai_in", [H, NS])
            d_row = sbo("d_row", [1, H])
            dt, eA = exps[:, 0:1], exps[:, 1:1 + NS]
            (are, are_arg, aim, exp_are, half_aim, arg_s, arg_c, sn, cs, em1, t1, t2, t3, zr, zi, inv) = (
                sbo(n, [H, NS]) for n in ("are", "are_arg", "aim", "exp_are", "half_aim", "arg_s", "arg_c", "sn",
                                          "cs", "em1", "t1", "t2", "t3", "zr", "zi", "inv"))
            par_h = sbo("par_h", [H, 4, 2, NS])
            par = sbo("par", [P, 4, H])
            (e_r, e_l, th_r, th_l, turns, s_r, p_1, p_2) = (
                sbo(n, [P, HC, 32]) for n in ("e_r", "e_l", "th_r", "th_l", "turns", "s_r", "p_1", "p_2"))
            right, left = th_r, th_l
            k_sb = sbo("k_sb", [32, HC, 32])
            zero = sbo("zero", [H, P])
            toep = sbo("toep", [P, TRING, L])
            x_in, x_rev = toep[:, 0:4, :], toep[:, 4:8, :]
            u_all = y_parts[:].bitcast(F32)
            u_t = sbo("u_t", [P, 2, KT, P])
            y_nat = sbo("y_nat", [P, 2, KT, P])

        for m in ("d0", "d1"):
            w_h[m] = sb(f"w{m}_h", [P, HID], F32R)
            w_l[m] = sb(f"w{m}_l", [P, HID], F32R)
            diff[m] = sb(f"diff_{m}", [P, HID], BF16)
        mid_h = sb("mid_h", [P, 2, HALF], F32R)
        mid_l = sb("mid_l", [P, 2, HALF], F32R)
        acc = sb("acc", [P, HALF // P, HID])
        silu = sb("silu", [P, 2, 512])
        mid = sb("mid", [P, 2, 512])
        qd_in = [sb(f"qd_in{e}", [P, HID], I32) for e in range(2)]
        sd_in = [sb(f"sd_in{e}", [P, HID], F16) for e in range(2)]
        zd_in = [sb(f"zd_in{e}", [P, HID // PACK], I32) for e in range(2)]
        z_one["d"] = sb("zd_one", [P, HID], BF16)
        x_fin = [silu, mid]
        ffn16 = sb("ffn16", [P, 2, HID], F16)

        par_in, tab_in, len_in, lens_in = sem("par_in"), sem("tab_in"), sem("len_in"), sem("lens_in")
        x_loaded = [sem(f"x_loaded{i}") for i in range(4)]
        logs_in, mask_ready, u_all_ready = sem("logs_in"), sem("mask_ready"), sem("u_all_ready")
        t_loaded = [sem(f"t_loaded{i}") for i in range(TRING)]
        y_stored = [sem("y_stored0"), sem("y_stored1")]
        k_stored, zero_stored, const_ready = sem("k_stored"), sem("zero_stored"), sem("const_ready")
        dve_step = sem("dve_step")
        f_args, f_done = sem("f_args"), sem("f_done")
        par_ready, par_turned = sem("par_ready"), sem("par_turned")
        lr_ready, k_mm, k_sb_ready = sem("lr_ready"), sem("k_mm"), sem("k_sb_ready")
        rev_ready, u_turned, u_ready = sem("rev_ready"), sem("u_turned"), sem("u_ready")
        conv_mm, y_ready = sem("conv_mm"), sem("y_ready")

        turn_ps = [bank[0:2], bank[2:4]]
        conv_ps = [bank[2:4], bank[4:6]]
        k_ps, par_ps = bank[6], bank[7]

        shifts_in = sem("shifts_in")
        y0_loaded = [sem(f"y0_loaded{k}") for k in range(KT)]
        y1_loaded = [sem(f"y1_loaded{k}") for k in range(KT)]
        y_cast, y_split = sem("y_cast"), sem("y_split")
        gu_in = {m: sem(f"{m}_in") for m in ("g", "u")}
        gu_used = {m: sem(f"{m}_used") for m in ("g", "u")}
        d_in = [sem(f"d_in{e}") for e in range(2)]
        x_fin_in = [sem("x_fin_in0"), sem("x_fin_in1")]
        ffn16_ready, out_ready, out_stored = sem("ffn16_ready"), sem("out_ready"), sem("out_stored")
        diff_ready, full_ready, high_ready, slot_ready = (
            sem("diff_ready"), sem("full_ready"), sem("high_ready"), sem("slot_ready"))
        g_mm, u_mm, d_mm = sem("g_mm"), sem("u_mm"), sem("d_mm")
        silu_done, mid_done, mid_cast, mid_ready, acc_done = (
            sem("silu_done"), sem("mid_done"), sem("mid_cast"), sem("mid_ready"), sem("acc_done"))

        g_ps, u_ps, d_ps = bank[0:2], bank[2:4], bank[4:8]

        ORDER = ["g", "d0", "d1", "u", "g", "u"]
        NLOAD = 3
        TT = HALF // P

        def x_rows(g):
            return bass.AP(x.tensor, g * (HG * L), [[L, HG], [H * L, B], [1, L]])

        block = ctx.enter_context(nc.Block())

        @block.sync
        def _(sp):
            src = {"g": (gq, gs, gz), "u": (uq, us, uz)}

            def load_gu(m, n0, width, number):
                q, s, z = src[m]
                sp.wait_ge(gu_used[m], number + 1)
                sp.dma_start(q_in[m][:, 0:width], q[:, n0:n0 + width]).then_inc(gu_in[m], 16)
                sp.dma_start(s_in[m][:, 0:width],
                             bass.AP(s.tensor, n0, [[INTER, 8], [0, 16], [1, width]])).then_inc(gu_in[m], 16)
                sp.dma_start(z_in[m][:, 0:width // PACK],
                             bass.AP(z.tensor, n0 // PACK, [[INTER // PACK, 8], [0, 16], [1, width // PACK]])
                             ).then_inc(gu_in[m], 16)

            for y in y_stored:
                sp.sem_inc(y, 16)
            sp.dma_start(logs[:, 0:1], log_dt.rearrange("(h o) -> h o", o=1)).then_inc(logs_in, 16)
            sp.dma_start(logs[:, 1:1 + NS], log_A).then_inc(logs_in, 16)
            sp.dma_start(len_i[:], bass.AP(itok.tensor, 0, [[0, HG], [1, B], [1, 1]])).then_inc(len_in, 16)
            sp.dma_start(ai_in[:], A_imag).then_inc(par_in, 16)
            sp.dma_start(x_in[:, 0, :], x_rows(0)).then_inc(x_loaded[0], 16)
            sp.dma_start(ident[:], ident_in).then_inc(tab_in, 16)
            sp.dma_start(c_in[:], C).then_inc(par_in, 16)
            sp.dma_start(d_row[:], D.rearrange("(o h) -> o h", o=1)).then_inc(par_in, 16)
            sp.dma_start(tab[:], ctab).then_inc(tab_in, 16)
            sp.dma_start(lens_i[:], bass.AP(itok.tensor, 0, [[0, P], [1, B]])).then_inc(lens_in, 16)
            for g in range(1, 4):
                sp.dma_start(x_in[:, g, :], x_rows(g)).then_inc(x_loaded[g], 16)
            with sp.Fori(1, NG // 4) as i:
                for j in range(4):
                    sp.wait_ge(rev_ready, i * 4 + (j - 3))
                    sp.dma_start(x_in[:, j, :], x_rows(i * 4 + j)).then_inc(x_loaded[j], 16)
            sp.wait_ge(zero_stored, 16)

            def store_kernels(hc):
                dst = bass.AP(kpad.tensor, hc * (HC * KPAD) + P, [[32, 32], [KPAD, HC], [1, 32]])
                sp.dma_start(dst, k_sb[:]).then_inc(k_stored, 16)

            def load_toeplitz(g, half_):
                for hh in range(HG):
                    slot = HG * half_ + hh
                    sp.wait_ge(conv_mm, g * HG + (hh + 1))
                    src = bass.AP(kpad.tensor, (g * HG + hh) * KPAD + 1, [[1, P], [1, L]])
                    sp.dma_start(toep[:, slot, :], src).then_inc(t_loaded[slot], 16)

            def piece(hc, last):
                for q in range(4):
                    g = hc * 4 + q
                    if q == 2 and not last:
                        sp.wait_ge(k_sb_ready, hc + 3)
                        store_kernels(hc + 1)
                        sp.wait_ge(k_stored, hc * 16 + 32)
                    if not (last and q >= 2):
                        load_toeplitz(g + 2, q % 2)
                    sp.wait_ge(y_ready, g * 2 + 6)
                    dst = bass.AP(ysc.tensor, g * P, [[TOK, P], [P * TOK, KT], [1, P]])
                    sp.dma_start(dst, y_nat[:, q % 2, :, :]).then_inc(y_stored[q % 2], 16)

            sp.wait_ge(k_sb_ready, 2)
            store_kernels(0)
            sp.wait_ge(rev_ready, NG)
            sp.wait_ge(k_stored, 16)
            load_toeplitz(0, 0)
            sp.wait_ge(u_turned, NG + 4)
            load_toeplitz(1, 1)
            sp.dma_start(shifts[:], stab).then_inc(shifts_in, 16)
            load_gu("g", 0, 1024, 0)
            load_gu("u", 0, 1024, 0)
            with sp.Fori(0, NHC - 1) as hc:
                piece(hc, False)
            piece(NHC - 1, True)
            for y in y_stored:
                sp.wait_ge(y, 16 + 16 * NG // 2)

            def load_down(c, e, number):
                sp.wait_ge(full_ready, number * 6 + (4 + e))
                if c < NT:
                    t, n, G = c // 4, P, HID // PACK
                    q_src = dq[P * t:P * t + P, :]
                    s_src = bass.AP(ds.tensor, 8 * t * HID, [[HID, 8], [0, 16], [1, HID]])
                    z_src = bass.AP(dz.tensor, 8 * t * G, [[G, 8], [0, 16], [1, G]])
                else:
                    v = 2 * (c - NT) + e
                    n, G = (P if 2 * c + e < 2 * NC - 1 else LAST), HID // PACK
                    q_src = bass.AP(dq.tensor, (256 + 16 * v) * HID, [[HID, n // 8], [0, 8], [1, HID]])
                    s_src = bass.AP(ds.tensor, (16 + v) * HID, [[0, n], [1, HID]])
                    z_src = bass.AP(dz.tensor, (16 + v) * G, [[0, n], [1, G]])
                sp.dma_start(qd_in[e][0:n, :], q_src).then_inc(d_in[e], 16)
                sp.dma_start(sd_in[e][0:n, :], s_src).then_inc(d_in[e], 16)
                sp.dma_start(zd_in[e][0:n, :], z_src).then_inc(d_in[e], 16)

            for e in range(2):
                load_down(0, e, 0)
            with sp.Fori(0, 2) as hf:
                for c in range(NC):
                    for e in range(2):
                        load_down((c + 1) % NC, e, hf * NC + (c + 1))
                    if c in (3, 7, NC - 1):
                        n0, width = {3: (1024, 1024), 7: (2048, INTER - 2048), NC - 1: (0, 1024)}[c]
                        number = {3: 1, 7: 2, NC - 1: 3}[c]
                        for m in ("g", "u"):
                            load_gu(m, n0, width, hf * NLOAD + number)
                sp.wait_ge(mid_ready, (hf + 1) * (4 * NC))
                for tt in range(2):
                    sp.dma_start(x_fin[tt][:], x_rows(hf * TT + tt)).then_inc(x_fin_in[tt], 16)
                for tt in range(TT):
                    sp.wait_ge(out_ready, hf * TT + (TT + tt + 1))
                    if tt + 2 < TT:
                        sp.dma_start(x_fin[tt % 2][:], x_rows(hf * TT + (tt + 2))).then_inc(x_fin_in[tt % 2], 16)
                    dst = bass.AP(out.tensor, (hf * TT + tt) * (HG * L), [[L, HG], [H * L, B], [1, L]])
                    sp.dma_start(dst, acc[:, tt, :]).then_inc(out_stored, 16)
            sp.wait_ge(out_stored, 16 + 16 * 2 * TT)
            for e in range(2):
                sp.wait_ge(d_in[e], 48 * (2 * NC + 1))
            for m in ("g", "u"):
                sp.wait_ge(gu_in[m], 48 * (2 * NLOAD + 1))

        @block.gpsimd
        def _(pool):
            pool.iota(iota_l[:], [[1, L]], base=0, channel_multiplier=0,
                      allow_small_or_imprecise_dtypes=True).then_inc(const_ready, 1)
            pool.memset(zero[:], 0.0).then_inc(const_ready, 1)
            pool.wait_ge(const_ready, 2)
            pool.dma_start(kpad[:, 0:P], zero[:]).then_inc(zero_stored, 16)
            pool.wait_ge(mask_ready, 1)
            with pool.Fori(0, POOL_G // 4) as i:
                for j in range(4):
                    pool.wait_ge(x_loaded[j], i * 16 + 16)
                    pool.wait_ge(u_turned, i * 4 + (j + 1))
                    pool.tensor_tensor(x_rev[:, j, :].rearrange("p (c l) -> p c l", c=KT)[:, :, ::-1],
                                       x_in[:, j, :].rearrange("p (c l) -> p c l", c=KT),
                                       mask_row[:].rearrange("p (c l) -> p c l", c=KT), ALU.mult
                                       ).then_inc(rev_ready, 1)
            for y in y_stored:
                pool.wait_ge(y, 16 + 16 * NG // 4)
            for k in range(KT):
                kt = k // 2 + 4 * (k % 2)
                pool.wait_ge(conv_mm, TRING + 46 + k)
                src = bass.AP(ysc.tensor, kt * TOK, [[PACK * TOK, P], [1, HALF]])
                pool.dma_start(y_l[:, kt, :].bitcast(F32), src).then_inc(y0_loaded[k], 16)

            pool.sem_inc(full_ready, 6)
            pool.sem_inc(slot_ready, 2)

            def multiply(m, parity, number, n=P):
                pool.wait_ge(diff_ready, number)
                pool.wait_ge(slot_ready, number)
                if m in ("g", "u"):
                    dst = w_full[:, parity, :].rearrange("p (a b r) -> p a b r", a=4, b=2)
                    src = diff[m][:].rearrange("p (a r b) -> p a b r", a=4, b=2)
                    sc = bass.AP(s_tile[m][:].tensor, 0, [[P, P], [0, 4], [0, 2], [1, P]])
                    pool.tensor_tensor(dst, src, sc, ALU.mult).then_inc(full_ready, 1)
                else:
                    pool.tensor_tensor(w_full[0:n, parity, :], diff[m][0:n, :], sd_in[int(m[1])][0:n, :],
                                       ALU.mult).then_inc(full_ready, 1 if n == P else 2)

            def low(m, parity, number, n=P):
                pool.wait_ge(high_ready, number)
                if n < P:
                    pool.wait_ge(slot_ready, number + 1)
                dst = w_l[m][:] if n == P else w_h[m][n:2 * n, :]
                pool.tensor_tensor(dst, w_full[0:n, parity, :], w_h[m][0:n, :].bitcast(F32), ALU.subtract
                                   ).then_inc(slot_ready, 1 if n == P else 2)

            def tiles(last, chunk):
                def rows(k):
                    return LAST if last and k == 2 else P

                def low_before(k):
                    if not (last and k == 4):
                        low(ORDER[k - 1], (k - 1) % 2, chunk * 6 + (k + 2), n=rows(k - 1))

                for k, m in enumerate(ORDER):
                    if k == 4:
                        low_before(k)
                    if not (last and k == 3):
                        multiply(m, k % 2, chunk * 6 + (k + 3), n=rows(k))
                    if k not in (0, 4):
                        low_before(k)

            multiply("g", 0, 1)
            multiply("u", 1, 2)
            low("g", 0, 1)
            with pool.Fori(0, 2) as hf:
                for k in range(KT):
                    kt = k // 2 + 4 * (k % 2)
                    pool.wait_ge(y_cast, hf * KT + (k + 1))
                    pool.tensor_tensor(y_l[:, kt, :], y_l[:, kt, :].bitcast(F32), y_h[:, kt, :].bitcast(F32),
                                       ALU.subtract).then_inc(y_split, 1)
                low("u", 1, hf * (6 * NC) + 2)
                with pool.Fori(0, NC - 1) as c:
                    tiles(False, hf * NC + c)
                    low("u", 1, (hf * NC + c) * 6 + 8)
                tiles(True, hf * NC + (NC - 1))

        @block.scalar
        def _(act):
            act.sem_inc(u_all_ready, 4)
            act.sem_inc(silu_done, 1)
            act.sem_inc(out_stored, 16)
            act.wait_ge(f_args, 1)
            act.activation(exp_are[:], are_arg[:], ACT.Exp).then_inc(f_done, 1)
            act.wait_ge(f_args, 2)
            act.activation(sn[:], arg_s[:], ACT.Sin).then_inc(f_done, 1)
            act.wait_ge(f_args, 3)
            act.activation(cs[:], arg_c[:], ACT.Sin).then_inc(f_done, 1)

            def functions_right(hc):
                act.wait_ge(f_args, hc * 5 + 4)
                act.activation(e_r[:], e_r[:], ACT.Exp).then_inc(f_done, 1)
                act.wait_ge(f_args, hc * 5 + 5)
                act.activation(e_l[:], e_l[:], ACT.Exp).then_inc(f_done, 1)
                act.wait_ge(f_args, hc * 5 + 6)
                act.activation(s_r[:], s_r[:], ACT.Sin).then_inc(f_done, 1)

            def functions_left(hc):
                act.wait_ge(f_args, hc * 5 + 7)
                act.activation(p_1[:], p_1[:], ACT.Sin).then_inc(f_done, 1)
                act.wait_ge(f_args, hc * 5 + 8)
                act.activation(p_2[:], p_2[:], ACT.Sin, bias=tab[:, C_NHPI:C_NHPI + 1]).then_inc(f_done, 1)

            def take_turned(i):
                for j in range(2):
                    act.wait_ge(u_turned, i * 2 + (j + 5))
                    for k in range(2):
                        dst = bass.AP(u_all.tensor, i * (2 * L) + (j * L + 512 * k), [[2 * KT * HALF, P], [1, 512]])
                        act.copy(dst, turn_ps[j][k][:]).then_inc(u_all_ready, 1)

            def bring(g, half_):
                act.wait_ge(conv_mm, g * HG + 4)
                src = bass.AP(u_all.tensor, g * L, [[2 * KT * HALF, P], [1, L]])
                act.copy(u_t[:, half_, :, :].rearrange("p c r -> p (c r)"), src).then_inc(u_ready, 1)

            def high(m, parity, number, n=P):
                act.wait_ge(full_ready, number + 6)
                act.copy(w_h[m][0:n, :], w_full[0:n, parity, :]).then_inc(high_ready, 1 if n == P else 2)

            def take_gate(chunk, e, fused=False):
                if fused:
                    act.wait_ge(u_mm, chunk * 2 + 3)
                else:
                    act.wait_ge(g_mm, chunk * 2 + (e + 1))
                act.wait_ge(mid_done, chunk * 4 + (2 * e + 1))
                M0, M = (LAST, LAST) if fused else (0, P)
                for tb in range(2):
                    ins = act.activation(silu[M0:M0 + M, tb, :], g_ps[tb][0:M, :], ACT.Silu)
                ins.then_inc(silu_done, 1)

            def cast_mid(chunk, e, fused=False):
                for tb in range(2):
                    act.wait_ge(mid_done, chunk * 4 + (2 * e + tb + 2))
                    for M0 in (0, LAST) if fused else (0,):
                        M = LAST if fused else P
                        ins = act.copy(mid_h[M0:M0 + M, e, 512 * tb:512 * tb + 512], mid[0:M, tb, :])
                    ins.then_inc(mid_cast, 1)

            def body(last, chunk, load_y=False):
                take_gate(chunk, 0)
                act.wait_ge(g_mm, chunk * 2 + 1)
                high("g", 0, chunk * 6 + 3)
                act.wait_ge(acc_done, chunk * 16 + 4)
                high("d0", 1, chunk * 6 + 4)
                high("d1", 0, chunk * 6 + 5, n=LAST if last else P)
                if not last:
                    act.wait_ge(u_mm, chunk * 2 + 2)
                    high("u", 1, chunk * 6 + 6)
                cast_mid(chunk, 0)
                take_gate(chunk, 1, fused=last)
                act.wait_ge(u_mm if last else g_mm, chunk * 2 + (3 if last else 2))
                high("g", 0, chunk * 6 + 7)
                cast_mid(chunk, 1, fused=last)
                if load_y:
                    act.wait_ge(u_mm, 2 * NC + 1)
                    for k, kt in enumerate(order):
                        src = bass.AP(ysc.tensor, HALF + kt * TOK, [[PACK * TOK, P], [1, HALF]])
                        act.dma_start(y_l[:, kt, :].bitcast(F32), src).then_inc(y1_loaded[k], 16)
                act.wait_ge(u_mm, chunk * 2 + 3)
                high("u", 1, chunk * 6 + 8)

            order = [k // 2 + 4 * (k % 2) for k in range(KT)]

            def cast_y(k, loaded):
                act.wait_ge(loaded[k], 16)
                act.copy(y_h[:, order[k], :], y_l[:, order[k], :].bitcast(F32)).then_inc(y_cast, 1)

            def piece(hc, last):
                for q in range(4):
                    g = hc * 4 + q
                    if not (last and q == 3):
                        bring(g + 1, (q + 1) % 2)
                    if not last and q == 0:
                        functions_right(hc + 1)
                    if not last and q == 1:
                        functions_left(hc + 1)
                    if last:
                        if q == 1:
                            high("g", 0, 1)
                        if q == 2:
                            high("u", 1, 2)
                        act.wait_ge(u_ready, min(g + 2, NG))
                        for k in ((), (0, 1), (2, 3, 4, 5), (6, 7))[q]:
                            cast_y(k, y0_loaded)

            act.wait_ge(tab_in, 32)
            with act.Fori(0, 3) as i:
                take_turned(i)
            functions_right(0)
            functions_left(0)
            with act.Fori(3, NG // 2) as i:
                take_turned(i)
            act.wait_ge(u_all_ready, 2 * NG + 4)
            bring(0, 0)
            with act.Fori(0, NHC - 1) as hc:
                piece(hc, False)
            piece(NHC - 1, True)
            for y in y_stored:
                act.wait_ge(y, 16 + 16 * NG // 2)

            def finish(hf, tt):
                act.wait_ge(acc_done, hf * (16 * NC) + (16 * (NC - 1) + 2 * tt + 6))
                act.wait_ge(out_ready, hf * TT + (TT + tt - 1))
                act.copy(ffn16[:, tt % 2, :], acc[:, tt, :]).then_inc(ffn16_ready, 1)

            for hf in range(2):
                with act.Fori(0, NC - 1) as c:
                    body(False, c + hf * NC)
                body(True, hf * NC + (NC - 1), load_y=hf == 0)
                if hf == 0:
                    for k in range(3):
                        cast_y(k, y1_loaded)
                for tt in range(TT):
                    if hf == 0 and tt + 3 < KT:
                        cast_y(tt + 3, y1_loaded)
                    finish(hf, tt)
                act.wait_ge(out_ready, (hf + 2) * TT)

        @block.vector
        def _(dve):
            step = Count(dve_step)

            def do(*steps):
                for ins in steps:
                    step.inc(ins)
                dve.wait_ge(dve_step, step.value())

            def col(i):
                return tab[:, i:i + 1]

            dve.sem_inc(lr_ready, 1)
            dve.sem_inc(k_sb_ready, 1)
            dve.sem_inc(y_ready, 4)
            for m in ("g", "u"):
                dve.sem_inc(gu_used[m], 1)
            dve.sem_inc(mid_done, 1)
            dve.sem_inc(acc_done, 4)
            dve.sem_inc(out_ready, TT)
            dve.wait_ge(len_in, 16)
            do(dve.tensor_copy(len_col[:], len_i[:]))
            dve.wait_ge(const_ready, 1)
            dve.tensor_scalar(mask_row[:], iota_l[:], len_col[:, 0:1], None, ALU.is_lt).then_inc(mask_ready, 1)
            dve.wait_ge(logs_in, 32)

            def times(out_, a_, b_):
                return dve.tensor_tensor(out_, a_, b_, ALU.mult)

            def fma(out_, a_, c, b_):
                return dve.scalar_tensor_tensor(out=out_, in0=a_, scalar=c, in1=b_, op0=ALU.mult, op1=ALU.add)

            def series(p, r):
                yield dve.tensor_scalar(p, r, 1 / 5040.0, None, ALU.mult)
                for c in (1 / 720.0, 1 / 120.0, 1 / 24.0, 1 / 6.0, 0.5, 1.0):
                    yield dve.scalar_tensor_tensor(out=p, in0=p, scalar=c, in1=r, op0=ALU.add, op1=ALU.mult)

            do(dve.tensor_scalar(logs[:], logs[:], -87.0, 88.0, ALU.max, ALU.min))
            do(dve.tensor_scalar(power[:], logs[:], 1 / LN2, None, ALU.mult))
            do(dve.tensor_scalar(power[:], power[:], MAGIC, MAGIC, ALU.add, ALU.subtract))
            do(fma(rest[:], power[:], -LN2_1, logs[:]), dve.tensor_scalar(power_i[:], power[:], 127.0, None, ALU.add))
            do(fma(rest[:], power[:], -LN2_2, rest[:]),
               dve.tensor_scalar(power_i[:], power_i[:], 23, None, ALU.logical_shift_left))
            for ins in series(exps[:], rest[:]):
                do(ins)
            do(dve.scalar_tensor_tensor(out=exps[:], in0=exps[:], scalar=1.0, in1=power_i[:].bitcast(F32),
                                        op0=ALU.add, op1=ALU.mult))
            dve.wait_ge(par_in, 48)
            dve.wait_ge(tab_in, 32)
            do(dve.tensor_scalar(are[:], eA, dt, -1.0, ALU.mult, ALU.mult),
               dve.tensor_scalar(aim[:], ai_in[:], dt, None, ALU.mult),
               times(inv[:], eA, eA), times(t3[:], ai_in[:], ai_in[:]))
            dve.tensor_copy(are_arg[:], are[:]).then_inc(f_args, 1)
            do(dve.tensor_scalar(half_aim[:], aim[:], 0.5, None, ALU.mult),
               dve.tensor_scalar(t2[:], are[:], -0.25, 0.25, ALU.max, ALU.min),
               dve.tensor_tensor(inv[:], inv[:], t3[:], ALU.add))
            poly = series(em1[:], t2[:])
            do(dve.tensor_scalar(t1[:], half_aim[:], 1 / TWO_PI, None, ALU.mult),
               dve.tensor_scalar(zr[:], half_aim[:], 1 / TWO_PI, 0.25, ALU.mult, ALU.add),
               dve.reciprocal(inv[:], inv[:]), next(poly))
            do(dve.tensor_scalar(t1[:], t1[:], MAGIC, MAGIC, ALU.add, ALU.subtract),
               dve.tensor_scalar(zr[:], zr[:], MAGIC, MAGIC, ALU.add, ALU.subtract), next(poly))
            do(fma(arg_s[:], t1[:], -PI1, half_aim[:]), fma(arg_c[:], zr[:], -PI1, half_aim[:]), next(poly))
            do(fma(arg_s[:], t1[:], -PI2, arg_s[:]), fma(arg_c[:], zr[:], -PI2, arg_c[:]), next(poly))
            do(fma(arg_s[:], t1[:], -PI3, arg_s[:]), fma(arg_c[:], zr[:], -PI3, arg_c[:]), next(poly))
            do(dve.tensor_scalar(arg_c[:], arg_c[:], 0.25 * TWO_PI, PI_BELOW, ALU.add, ALU.min), next(poly))
            dve.tensor_scalar(arg_s[:], arg_s[:], -PI_BELOW, PI_BELOW, ALU.max, ALU.min).then_inc(f_args, 1)
            dve.tensor_scalar(arg_c[:], arg_c[:], -PI_BELOW, None, ALU.max).then_inc(f_args, 1)
            do(next(poly))
            dve.wait_ge(f_done, 1)
            do(dve.tensor_scalar(t1[:], exp_are[:], 1.0, None, ALU.subtract),
               dve.tensor_tensor(half_aim[:], t2[:], are[:], ALU.is_equal))
            do(times(em1[:], em1[:], half_aim[:]), dve.tensor_scalar(zi[:], half_aim[:], -1.0, 1.0, ALU.mult, ALU.add))
            do(times(t1[:], t1[:], zi[:]))
            dve.wait_ge(f_done, 3)
            do(dve.tensor_tensor(em1[:], em1[:], t1[:], ALU.add),
               dve.scalar_tensor_tensor(out=t3[:], in0=sn[:], scalar=-2.0, in1=sn[:], op0=ALU.mult, op1=ALU.mult),
               dve.scalar_tensor_tensor(out=zr[:], in0=sn[:], scalar=2.0, in1=cs[:], op0=ALU.mult, op1=ALU.mult))
            do(dve.scalar_tensor_tensor(out=t2[:], in0=t3[:], scalar=1.0, in1=em1[:], op0=ALU.add, op1=ALU.mult),
               times(zr[:], zr[:], exp_are[:]))
            do(dve.tensor_tensor(t1[:], t3[:], t2[:], ALU.add))
            do(times(arg_s[:], zr[:], ai_in[:]), times(t3[:], t1[:], eA),
               times(arg_c[:], zr[:], eA), times(t2[:], t1[:], ai_in[:]))
            do(dve.tensor_tensor(zr[:], arg_s[:], t3[:], ALU.subtract),
               dve.scalar_tensor_tensor(out=zi[:], in0=arg_c[:], scalar=-1.0, in1=t2[:], op0=ALU.mult,
                                        op1=ALU.subtract))
            do(times(zr[:], zr[:], inv[:]), times(zi[:], zi[:], inv[:]))
            cr, ci = c_in[:, :, 0], c_in[:, :, 1]
            do(times(t1[:], cr, zr[:]), times(t2[:], ci, zi[:]), times(t3[:], cr, zi[:]), times(em1[:], ci, zr[:]))
            do(dve.tensor_tensor(t1[:], t1[:], t2[:], ALU.subtract), dve.tensor_tensor(t3[:], t3[:], em1[:], ALU.add))
            for n in range(2):
                dve.tensor_copy(par_h[:, 0, n, :], are[:]).then_inc(par_ready, 1)
                dve.tensor_copy(par_h[:, 1, n, :], aim[:]).then_inc(par_ready, 1)
                dve.tensor_scalar(par_h[:, 2, n, :], t1[:], 2.0, None, ALU.mult).then_inc(par_ready, 1)
                dve.tensor_scalar(par_h[:, 3, n, :], t3[:], 2.0, None, ALU.mult).then_inc(par_ready, 1)
            dve.wait_ge(par_turned, 1)
            do(dve.tensor_copy(par[:], par_ps[:, 0:4 * H].rearrange("p (v h) -> p v h", v=4)))

            def wide(v, hc):
                return bass.AP(par[:].tensor, hc * HC + v * H, [[4 * H, P], [1, HC], [0, 32]])

            def exponents(c0):
                return bass.AP(tab[:].tensor, c0, [[C_N, P], [0, HC], [1, 32]])

            def arguments(hc):
                dve.wait_ge(lr_ready, hc + 1)
                dve.wait_ge(k_mm, hc + 1)
                dve.tensor_tensor(e_r[:], wide(0, hc), exponents(C_B), ALU.mult).then_inc(f_args, 1)
                dve.tensor_tensor(e_l[:], wide(0, hc), exponents(C_A), ALU.mult).then_inc(f_args, 1)
                dve.tensor_tensor(th_r[:], wide(1, hc), exponents(C_B), ALU.mult)
                do(dve.tensor_tensor(th_l[:], wide(1, hc), exponents(C_A), ALU.mult))

            def reduce(arg, th, off, off_t):
                do(dve.tensor_scalar(turns[:], th[:], 1 / TWO_PI, col(off_t), ALU.mult, ALU.add))
                do(dve.tensor_scalar(turns[:], turns[:], MAGIC, MAGIC, ALU.add, ALU.subtract))
                do(fma(arg[:], turns[:], -PI1, th[:]))
                do(fma(arg[:], turns[:], -PI2, arg[:]))
                do(fma(arg[:], turns[:], -PI3, arg[:]))
                do(dve.tensor_scalar(arg[:], arg[:], col(off), PI_BELOW, ALU.add, ALU.min))

            def reduce_right():
                reduce(s_r, th_r, C_OFFR, C_OFFR_T)
                dve.tensor_scalar(s_r[:], s_r[:], -PI_BELOW, None, ALU.max).then_inc(f_args, 1)

            def reduce_left():
                reduce(p_1, th_l, C_OFFL, C_OFFL_T)
                do(dve.tensor_scalar(p_1[:], p_1[:], -PI_BELOW, None, ALU.max))
                do(dve.scalar_tensor_tensor(out=p_2[:], in0=p_1[:], scalar=-1.0, in1=p_1[:], op0=ALU.mult, op1=ALU.max))
                dve.sem_inc(f_args, 2)

            def combine(hc):
                dve.wait_ge(f_done, hc * 5 + 8)
                dve.tensor_tensor(right[:], e_r[:], s_r[:], ALU.mult)
                do(dve.tensor_tensor(p_1[:], p_1[:], wide(2, hc), ALU.mult))
                do(dve.tensor_tensor(p_2[:], p_2[:], wide(3, hc), ALU.mult))
                do(dve.tensor_tensor(p_1[:], p_1[:], p_2[:], ALU.subtract))
                dve.tensor_tensor(left[:], p_1[:], e_l[:], ALU.mult).then_inc(lr_ready, 1)

            def take_kernel(hc):
                dve.wait_ge(k_mm, hc + 2)
                if not (isinstance(hc, int) and hc == 0):
                    dve.wait_ge(k_stored, hc * 16)
                do(dve.tensor_copy(k_sb[:], k_ps[0:32, :].rearrange("p (h b) -> p h b", h=HC)))
                d_piece = bass.AP(d_row[:].tensor, hc * HC, [[H, 1], [1, HC], [1, 1]])
                dve.tensor_tensor(k_sb[0:1, :, 0:1], k_sb[0:1, :, 0:1], d_piece, ALU.add).then_inc(k_sb_ready, 1)

            def mask_input(g):
                dve.wait_ge(x_loaded[g % 4], g // 4 * 16 + 16)
                dve.wait_ge(u_turned, g + 1)
                dve.tensor_tensor(x_rev[:, g % 4, :].rearrange("p (c l) -> p c l", c=KT)[:, :, ::-1],
                                  x_in[:, g % 4, :].rearrange("p (c l) -> p c l", c=KT),
                                  mask_row[:].rearrange("p (c l) -> p c l", c=KT), ALU.mult).then_inc(rev_ready, 1)

            def take_conv(g, half_):
                dve.wait_ge(y_stored[half_], (g - half_) * 8 + 16)
                for k in range(2):
                    dve.wait_ge(conv_mm, g * HG + (TRING + 2 * k + 2))
                    dve.tensor_tensor(
                        y_nat[:, half_, :, 64 * k:64 * k + 64].rearrange("p c (h b) -> p h c b", h=2),
                        conv_ps[half_][k][:].rearrange("p (h c b) -> p h c b", h=2, c=KT),
                        bass.AP(mask_t[:].tensor, 0, [[KT * B, P], [0, 2], [B, KT], [1, B]]),
                        ALU.mult).then_inc(y_ready, 1)

            def nibbles(dst, src_, a):
                return dve.tensor_scalar(dst, src_, 4 * a, 15, ALU.logical_shift_right, ALU.bitwise_and)

            def unpack_zeros(z, dst, n, width):
                words = z[0:n, 0:width // PACK].bitcast(U16).rearrange("p (m b) -> p m b", b=2)
                raw = dst[0:n, 0:width].bitcast(U16)
                for a in range(4):
                    ins = nibbles(raw.rearrange("p (m b a) -> p m b a", b=2, a=4)[:, :, :, a], words, a)
                do(ins)
                do(dve.tensor_scalar(dst[0:n, 0:width], raw, 1.0, None, ALU.add))

            def take_zeros(m, width, number):
                dve.wait_ge(gu_in[m], number * 48 + 48)
                unpack_zeros(z_in[m], z_one[m], P, width)

            def unpack_gu(m, c, e, full_count, last_use, into=None):
                m0, into = (0, m) if into is None else (LAST, into)
                if full_count is not None:
                    dve.wait_ge(full_ready, full_count)
                if c < NT:
                    i, M = c % 4 + 4 * e, P
                    words = q_in[m][:].bitcast(U16).rearrange("p (r i b) -> p r i b", i=8, b=2)[:, :, i, :]
                    zeros = bass.AP(z_one[m][:].tensor, i, [[1024, P], [0, 4], [8, P], [0, 2]])
                    scales = s_in[m][:].rearrange("p (r i) -> p r i", i=8)[:, :, i]
                else:
                    n0 = 256 * (c - NT) + P * e
                    M = P if 2 * c + e < 2 * NC - 1 else LAST
                    words = q_in[m][:, n0:n0 + M].bitcast(U16).rearrange("p (r b) -> p r b", b=2)
                    zeros = bass.AP(z_one[m][:].tensor, n0, [[1024, P], [0, 4], [1, M], [0, 2]])
                    scales = s_in[m][:, n0:n0 + M]
                whole = diff[into][:].rearrange("p (a r b) -> p a r b", a=4, b=2)[:, :, m0:m0 + M, :]
                for a in range(4):
                    nibbles(whole[:, a].bitcast(U16), words, a)
                ins = dve.tensor_copy(s_tile[into][:, m0:m0 + M], scales)
                if last_use is not None:
                    ins.then_inc(gu_used[m], 1)
                    dve.wait_ge(gu_used[m], last_use)
                else:
                    do(ins)
                ins = dve.tensor_tensor(whole, whole.bitcast(U16), zeros, ALU.subtract)
                if M == P or m0:
                    ins.then_inc(diff_ready, 1)

            def unpack_down(c, e, chunk):
                m, n = f"d{e}", (P if 2 * c + e < 2 * NC - 1 else LAST)
                dve.wait_ge(d_in[e], chunk * 48 + 48)
                dve.wait_ge(full_ready, chunk * 6 + (4 + e))
                dve.wait_ge(diff_ready, chunk * 6 + (3 + e))
                unpack_zeros(zd_in[e], z_one["d"], n, HID)
                q = qd_in[e][0:n, :]
                do(dve.tensor_scalar(q, q, shifts[0:n, 2 * c + e:2 * c + e + 1], 15,
                                     ALU.logical_shift_right, ALU.bitwise_and))
                dve.tensor_tensor(diff[m][0:n, :], q, z_one["d"][0:n, :], ALU.subtract
                                  ).then_inc(diff_ready, 1 if n == P else 2)

            def take_mid(c, e, chunk):
                M = P if 2 * c + e < 2 * NC - 1 else LAST
                k = chunk * 4 + 2 * e
                dve.wait_ge(u_mm, chunk * 2 + (e + 2))
                dve.wait_ge(silu_done, chunk * 2 + (e + 2))
                for tb in range(2):
                    if M == P:
                        dve.tensor_tensor(mid[:, tb, :], u_ps[tb][:], silu[:, tb, :], ALU.mult).then_inc(mid_done, 1)
                    else:
                        dve.tensor_tensor(mid[0:M, tb, :], g_ps[tb][M:P, :], silu[M:P, tb, :], ALU.mult
                                          ).then_inc(mid_done, 1)
                for tb in range(2):
                    dve.wait_ge(mid_cast, k + (tb + 1))
                    dve.wait_ge(mid_done, k + (tb + 2))
                    dve.tensor_tensor(mid_l[0:M, e, 512 * tb:512 * tb + 512], mid[0:M, tb, :],
                                      mid_h[0:M, e, 512 * tb:512 * tb + 512].bitcast(F32), ALU.subtract
                                      ).then_inc(mid_ready, 1)
                dve.wait_ge(mid_ready, k + 2)

            def add_down(c, chunk, i):
                tt, mb = i // 2, i % 2
                dst = acc[:, tt, 512 * mb:512 * mb + 512]
                dve.wait_ge(d_mm, chunk * 16 + (i + 1))
                if c == 0:
                    dve.tensor_copy(dst, d_ps[i % 4][:]).then_inc(acc_done, 1)
                else:
                    dve.wait_ge(acc_done, chunk * 16 + (i + 5 - 16))
                    dve.tensor_tensor(dst, d_ps[i % 4][:], dst, ALU.add).then_inc(acc_done, 1)

            arguments(0)
            reduce_right()
            reduce_left()
            dve.wait_ge(lens_in, 16)
            do(dve.tensor_copy(lens[:], lens_i[:]))
            for c in range(KT):
                dve.tensor_scalar(mask_t[:, c, :], lens[:], col(C_LCOL + c), None, ALU.is_gt)
            combine(0)
            dve.wait_ge(rev_ready, POOL_G)
            mask_input(POOL_G)
            mask_input(POOL_G + 1)
            take_kernel(0)
            for g in range(POOL_G + 2, NG):
                mask_input(g)

            def piece(hc, last):
                for q in range(4):
                    g = hc * 4 + q
                    if q == 0 and not last:
                        arguments(hc + 1)
                        reduce_right()
                    if q == 1 and not last:
                        reduce_left()
                    if q == 2 and not last:
                        take_kernel(hc + 1)
                    if q == 1 and not last:
                        combine(hc + 1)
                    take_conv(g, q % 2)
                    if last and q < 2:
                        m = "gu"[q]
                        take_zeros(m, 1024, 0)
                        unpack_gu(m, 0, 0, None, None)

            with dve.Fori(0, NHC - 1) as hc:
                step.enter(hc, CONV_STEPS)
                piece(hc, False)
                step.leave(NHC - 1)
            piece(NHC - 1, True)

            def finish(hf, tt):
                dve.wait_ge(x_fin_in[tt % 2], hf * (8 * TT) + 16 * (tt // 2 + 1))
                dve.wait_ge(ffn16_ready, hf * TT + (tt + 1))
                x_tile = x_fin[tt % 2][:].rearrange("p a b -> p (a b)")
                dve.tensor_tensor(acc[:, tt, :], x_tile, ffn16[:, tt % 2, :], ALU.add).then_inc(out_ready, 1)

            dve.wait_ge(shifts_in, 16)
            with dve.Fori(0, 2) as hf:
                step.enter(hf, FFN_STEPS)
                for c in range(NC):
                    chunk = hf * NC + c
                    load = {3: 0, 7: 1, NC - 1: 2}.get(c)
                    used = None if load is None else hf * NLOAD + (load + 2)
                    width = {3: 1024, 7: INTER - 2048, NC - 1: 1024}.get(c)
                    last = c == NC - 1
                    unpack_gu("g", c, 1, chunk * 6 + 7, used)
                    if last:
                        unpack_gu("u", c, 1, None, used, into="g")
                    if c == 1:
                        dve.wait_ge(out_stored, hf * (16 * TT) + 16)
                    for i in range(16):
                        if c:
                            add_down(c - 1, chunk - 1, i)
                        if i in (3, 8):
                            unpack_down(c, i // 8, chunk)
                        if i == 12 and not last:
                            unpack_gu("u", c, 1, chunk * 6 + 8, used)
                    take_mid(c, 0, chunk)
                    if load is not None:
                        take_zeros("g", width, hf * NLOAD + (load + 1))
                    unpack_gu("g", (c + 1) % NC, 0, chunk * 6 + 9, None)
                    if load is not None:
                        take_zeros("u", width, hf * NLOAD + (load + 1))
                    unpack_gu("u", (c + 1) % NC, 0, chunk * 6 + 12, None)
                    take_mid(c, 1, chunk)
                for i in range(16):
                    add_down(NC - 1, hf * NC + (NC - 1), i)
                    if i % 2 == 1 and i > 1:
                        finish(hf, i // 2 - 1)
                finish(hf, TT - 1)
                dve.wait_ge(out_ready, hf * TT + 2 * TT)
                step.leave(2)

        @block.tensor
        def _(pe):
            pe.sem_inc(k_mm, 1)
            pe.sem_inc(u_mm, 1)
            pe.sem_inc(u_turned, 4)
            pe.sem_inc(conv_mm, TRING)
            pe.wait_ge(tab_in, 32)

            def turn(g, j):
                pe.wait_ge(rev_ready, g + 1)
                pe.wait_ge(u_all_ready, g * 2 + 2)
                for c in range(KT):
                    mm = pe.transpose(turn_ps[j % 2][c // 4][:, P * (c % 4):P * (c % 4) + P],
                                      x_rev[:, j, P * c:P * c + P], ident[:])
                mm.then_inc(u_turned, 1)

            for g in range(4):
                turn(g, g)
            pe.wait_ge(par_ready, 8)
            for v in range(4):
                mm = pe.transpose(par_ps[:, v * H:(v + 1) * H], par_h[:, v, :, :].rearrange("p n s -> p (n s)"),
                                  ident[0:H, 0:H])
            mm.then_inc(par_turned, 1)
            with pe.Fori(1, POOL_G // 4) as i:
                for j in range(4):
                    turn(i * 4 + j, j)

            def multiply_kernel(hc):
                pe.wait_ge(lr_ready, hc + 2)
                pe.wait_ge(k_sb_ready, hc + 1)
                for h in range(HC):
                    mm = pe.matmul(k_ps[0:32, 32 * h:32 * h + 32], left[:, h, :], right[:, h, :],
                                   start=True, stop=True)
                mm.then_inc(k_mm, 1)

            def convolve(hc, q, last):
                g, half_ = hc * 4 + q, q % 2
                pe.wait_ge(u_ready, g + 1)
                for hh in range(HG):
                    if q == 2 and hh == 1 and not last:
                        multiply_kernel(hc + 1)
                    n = HG * q + hh
                    slot, k = n % TRING, hh // 2
                    pe.wait_ge(t_loaded[slot], hc * (16 * HC // TRING) + 16 * (n // TRING + 1))
                    if hh % 2 == 0:
                        pe.wait_ge(y_ready, g * 2 + (k + 1))
                    base = 256 * (hh % 2)
                    for d in range(KT):
                        mm = pe.matmul(
                            conv_ps[half_][k][:, base + B * d:base + 256],
                            toep[:, slot, P * d:P * d + P],
                            u_t[:, half_, 0:KT - d, B * hh:B * hh + B],
                            start=(d == 0), stop=(d == KT - 1))
                    mm.then_inc(conv_mm, 1)

            multiply_kernel(0)
            for g in range(POOL_G, NG):
                turn(g, g % 4)

            def piece(hc, last):
                for q in range(4):
                    convolve(hc, q, last)

            with pe.Fori(0, NHC - 1) as hc:
                piece(hc, False)
            piece(NHC - 1, True)

            def project(m, ps, count, hf=None, fused=False):
                mm = None
                for k in range(KT):
                    kt = k // 2 + 4 * (k % 2)
                    if hf is not None:
                        pe.wait_ge(y_split, hf * KT + (k + 1))
                    for w, ys in ((w_h[m], (y_h, y_l)), (w_l[m], (y_h,))):
                        for y in ys:
                            for tb in range(2):
                                before = mm
                                mm = pe.matmul(ps[tb][:], w[:, P * k:P * k + P], y[:, kt, 512 * tb:512 * tb + 512],
                                               start=(k == 0 and w is w_h[m] and y is y_h),
                                               stop=(k == KT - 1 and w is w_l[m]))
                if fused:
                    before.then_inc(g_mm, 1)
                mm.then_inc(count, 1)

            def gate(chunk, e, number, hf=None, fused=False):
                pe.wait_ge(slot_ready, number + 2)
                pe.wait_ge(silu_done, chunk * 2 + (e + 1))
                project("g", g_ps, u_mm if fused else g_mm, hf, fused)

            def up(chunk, e, number):
                pe.wait_ge(slot_ready, number + 2)
                pe.wait_ge(mid_done, chunk * 4 + (2 * e + 1))
                project("u", u_ps, u_mm)

            def down(chunk, last):
                pe.wait_ge(slot_ready, chunk * 6 + 7)
                if not last:
                    pe.wait_ge(mid_ready, chunk * 4 + 4)
                passes = [[(mid_h, w_h, P), (mid_h, w_l, P), (mid_l, w_h, P)] for e in range(2)]
                if last:
                    passes[1] = [(mid_h, w_h, P), (mid_l, w_h, LAST)]

                def output(i, e):
                    tt, mb = i // 2, i % 2
                    if e == 0:
                        pe.wait_ge(acc_done, chunk * 16 + (i + 1))
                    for j, (m_, w, n) in enumerate(passes[e]):
                        mm = pe.matmul(d_ps[i % 4][:], m_[0:n, e, P * tt:P * tt + P],
                                       w[f"d{e}"][0:n, 512 * mb:512 * mb + 512],
                                       start=(e == 0 and j == 0), stop=(e == 1 and j == len(passes[1]) - 1))
                    if e == 1:
                        mm.then_inc(d_mm, 1)

                ahead = 4 if last else 0
                if last:
                    pe.wait_ge(mid_ready, chunk * 4 + 2)
                    for i in range(ahead):
                        output(i, 0)
                    pe.wait_ge(mid_ready, chunk * 4 + 4)
                for i in range(16):
                    if i >= ahead:
                        output(i, 0)
                    output(i, 1)

            def rest_of(chunk, last):
                up(chunk, 0, chunk * 6 + 2)
                gate(chunk, 1, chunk * 6 + 3, fused=last)
                if not last:
                    up(chunk, 1, chunk * 6 + 6)

            pe.wait_ge(y_ready, 2 * NG + 2)
            with pe.Fori(0, 2) as hf:
                gate(hf * NC, 0, hf * (6 * NC) + 1, hf)
                rest_of(hf * NC, False)
                with pe.Fori(1, NC - 1) as c:
                    chunk = hf * NC + c
                    gate(chunk, 0, chunk * 6 + 1)
                    down(chunk - 1, False)
                    rest_of(chunk, False)
                chunk = hf * NC + (NC - 1)
                gate(chunk, 0, chunk * 6 + 1)
                down(chunk - 1, False)
                rest_of(chunk, True)
                down(chunk, True)


_INS = ["x", "itok_B_8_3872", "L0_cond_log_dt", "L0_cond_C", "L0_cond_log_A_real", "L0_cond_A_imag", "L0_cond_D",
        "L0_ffn_gate_qweight", "L0_ffn_gate_scales", "L0_ffn_gate_zeros",
        "L0_ffn_up_qweight", "L0_ffn_up_scales", "L0_ffn_up_zeros",
        "L0_ffn_down_qweight", "L0_ffn_down_scales", "L0_ffn_down_zeros"]


def kernel(**inputs):
    import concourse.bacc as _bacc
    from concourse.bass_utils import run_bass_kernel_spmd as _run

    nc = _bacc.Bacc("TRN2", target_bir_lowering=False, num_devices=1)
    arrays, args = {}, []

    def give(name, a):
        arrays[name] = a
        args.append(nc.dram_tensor(name, a.shape, mybir.dt.from_np(a.dtype), kind="ExternalInput").ap())

    for name in _INS:
        give(f"in_{name}_dram", np.ascontiguousarray(inputs[name]))
    give("const_table", const_table())
    give("shift_table", shift_table())
    give("identity", np.eye(P, dtype=np.float32))
    args.append(nc.dram_tensor("out_0_dram", (B, H, L), F32, kind="ExternalOutput").ap())
    build_program(nc, *args)
    r = _run(nc, [arrays], core_ids=[0])
    return r.results[0]["out_0_dram"]
```
